# Optimizing a Trainium2 kernel written in Bass

```python
import numpy as np
import jax
import jax.numpy as jnp

def _softmax(x, axis=-1):
    return jax.nn.softmax(x, axis=axis)

def _gelu(x):
    return jax.nn.gelu(x, approximate=True)

def _silu(x):
    return jax.nn.silu(x)

def _sigmoid(x):
    return jax.nn.sigmoid(x)

def _layernorm(x, axis=-1, eps=1e-05):
    m = jnp.mean(x, axis=axis, keepdims=True)
    v = jnp.var(x, axis=axis, keepdims=True)
    return (x - m) / jnp.sqrt(v + eps)

def _scatter_add(tgt, idx, src, axis=0):
    return tgt.at[idx].add(src)

def _segment_sum(src, seg, n):
    return jax.ops.segment_sum(src, seg, n)
kernel_name = 'mk_adj_resnorm_d4_adj_r2_e7fe7d'

def setup_inputs(seed: int=0):
    np.random.seed(seed)
    _w = jnp.asarray

    def _rec_inputs():
        import jax
        import jax.numpy as jnp
        _gk = jax.random.key(seed)
        x = -0.0005963 + 1.001 * jax.random.normal(jax.random.fold_in(_gk, 1), (2048, 256), jnp.float32)
        _a = jax.random.bernoulli(jax.random.fold_in(_gk, 2), 0.000976562, (2048, 2048))
        _a = jnp.logical_or(_a, jnp.swapaxes(_a, -1, -2))
        _a = jnp.logical_or(_a, jnp.eye(2048, dtype=bool))
        _af = _a.astype(jnp.float32)
        adj = _af
        return (x, adj)
    x, adj = _rec_inputs()

    def _L0_gnn_setup():
        import jax, jax.numpy as jnp
        import numpy as np
        N = 3072
        D_IN = 256
        D_OUT = 256
        DENSITY = 0.005
        key = jax.random.key(seed)
        ks = jax.random.split(key, 12)
        x = jax.random.normal(ks[0], (N, D_IN), dtype=jnp.float32)
        adj_a = (jax.random.uniform(ks[1], (N, N)) < DENSITY).astype(jnp.float32)
        adj_b = (jax.random.uniform(ks[2], (N, N)) < DENSITY).astype(jnp.float32)
        W_sa = jax.random.normal(ks[3], (D_IN, D_OUT), dtype=jnp.float32) * (1.414 / np.sqrt(D_IN + D_OUT))
        a_sa = jax.random.normal(ks[4], (1, 2 * D_OUT), dtype=jnp.float32) * (1.414 / np.sqrt(1 + 2 * D_OUT))
        stdv = 1.0 / np.sqrt(D_OUT)
        W_gcnb = jax.random.uniform(ks[5], (D_IN, D_OUT), minval=-stdv, maxval=stdv, dtype=jnp.float32)
        b_gcnb = jax.random.uniform(ks[6], (D_OUT,), minval=-stdv, maxval=stdv, dtype=jnp.float32)
        s = 1.0 / np.sqrt(2 * D_IN)
        Wa = jax.random.uniform(ks[7], (1, 2 * D_IN), minval=-s, maxval=s, dtype=jnp.float32)
        ba = jax.random.uniform(ks[8], (1,), minval=-s, maxval=s, dtype=jnp.float32)
        Wb = jax.random.uniform(ks[9], (1, 2 * D_IN), minval=-s, maxval=s, dtype=jnp.float32)
        bb = jax.random.uniform(ks[10], (1,), minval=-s, maxval=s, dtype=jnp.float32)
        return {'x': x, 'adj_a': adj_a, 'adj_b': adj_b, 'W_sa': W_sa, 'a_sa': a_sa, 'W_gcnb': W_gcnb, 'b_gcnb': b_gcnb, 'Wa': Wa, 'ba': ba, 'Wb': Wb, 'bb': bb}
    _L0_gnn_all = _L0_gnn_setup()
    _L0_gnn_in = {k: v for k, v in _L0_gnn_all.items() if k in ('W_sa', 'a_sa', 'W_gcnb', 'b_gcnb', 'Wa', 'ba', 'Wb', 'bb')}
    del _L0_gnn_all

    def _L1_gnn_setup():
        import jax, jax.numpy as jnp
        import numpy as np
        N = 4096
        D_IN = 256
        HEADS = 8
        DPH = 256 // HEADS
        EDGE_P = 0.01
        key = jax.random.key(seed)
        k1, k2, k3 = jax.random.split(key, 3)
        H = jax.random.normal(k1, (N, D_IN), dtype=jnp.float32)
        adj = (jax.random.uniform(k2, (N, N)) < EDGE_P).astype(jnp.float32)
        limit = float(np.sqrt(6.0 / (D_IN + DPH)))
        W = jax.random.uniform(k3, (HEADS, D_IN, DPH), jnp.float32, -limit, limit)
        b = jnp.zeros((HEADS, DPH), jnp.float32)
        return {'H': H, 'adj': adj, 'W': W, 'b': b}
    _L1_gnn_all = _L1_gnn_setup()
    _L1_gnn_in = {k: v for k, v in _L1_gnn_all.items() if k in ('W', 'b')}
    del _L1_gnn_all

    def _L2_gnn_setup():
        import jax, jax.numpy as jnp
        import numpy as np
        N = 4096
        IN_F = 256
        OUT_F = 256
        key = jax.random.key(seed)
        k1, k2, k3, k4 = jax.random.split(key, 4)
        input = jax.random.normal(k1, (N, IN_F), dtype=jnp.float32)
        adj = jax.random.uniform(k2, (N, N), dtype=jnp.float32)
        W = jax.random.normal(k3, (OUT_F, IN_F), dtype=jnp.float32) / np.sqrt(IN_F)
        b = jax.random.normal(k4, (OUT_F,), dtype=jnp.float32) * 0.01
        return {'input': input, 'adj': adj, 'W': W, 'b': b}
    _L2_gnn_all = _L2_gnn_setup()
    _L2_gnn_in = {k: v for k, v in _L2_gnn_all.items() if k in ('W', 'b')}
    del _L2_gnn_all

    def _L3_gnn_setup():
        import jax, jax.numpy as jnp
        import numpy as np
        EPS = 1e-08
        key = jax.random.key(seed)
        k1, k2, k3, k4 = jax.random.split(key, 4)
        N, IN, OUT = (4096, 256, 256)
        x = jax.random.normal(k1, (N, IN), dtype=jnp.float32)
        adj = jax.random.uniform(k2, (N, N), dtype=jnp.float32)
        W = jax.random.normal(k3, (OUT, IN), dtype=jnp.float32) * (1.0 / np.sqrt(IN))
        b = jax.random.normal(k4, (OUT,), dtype=jnp.float32) * 0.01
        return {'x': x, 'adj': adj, 'W': W, 'b': b}
    _L3_gnn_all = _L3_gnn_setup()
    _L3_gnn_in = {k: v for k, v in _L3_gnn_all.items() if k in ('W', 'b')}
    del _L3_gnn_all
    return {'x': x, 'adj': adj, 'L0_gnn_W_sa': _L0_gnn_in['W_sa'], 'L0_gnn_a_sa': _L0_gnn_in['a_sa'], 'L0_gnn_W_gcnb': _L0_gnn_in['W_gcnb'], 'L0_gnn_b_gcnb': _L0_gnn_in['b_gcnb'], 'L0_gnn_Wa': _L0_gnn_in['Wa'], 'L0_gnn_ba': _L0_gnn_in['ba'], 'L0_gnn_Wb': _L0_gnn_in['Wb'], 'L0_gnn_bb': _L0_gnn_in['bb'], 'L1_gnn_W': _L1_gnn_in['W'], 'L1_gnn_b': _L1_gnn_in['b'], 'L2_gnn_W': _L2_gnn_in['W'], 'L2_gnn_b': _L2_gnn_in['b'], 'L3_gnn_W': _L3_gnn_in['W'], 'L3_gnn_b': _L3_gnn_in['b']}

def reference(x, adj, L0_gnn_W_sa, L0_gnn_a_sa, L0_gnn_W_gcnb, L0_gnn_b_gcnb, L0_gnn_Wa, L0_gnn_ba, L0_gnn_Wb, L0_gnn_bb, L1_gnn_W, L1_gnn_b, L2_gnn_W, L2_gnn_b, L3_gnn_W, L3_gnn_b):
    import jax
    import jax.numpy as jnp

    def _L0_gnn_ref(x, adj_a, adj_b, W_sa, a_sa, W_gcnb, b_gcnb, Wa, ba, Wb, bb):
        import jax, jax.numpy as jnp
        import numpy as np
        N = 3072
        D_IN = 256
        D_OUT = 256
        DENSITY = 0.005
        type_sum_a = adj_a @ x
        type_sum_b = adj_b @ x
        attn_a = jax.nn.sigmoid(jnp.concatenate([type_sum_a, x], axis=1) @ Wa.T + ba)
        attn_b = jax.nn.sigmoid(jnp.concatenate([type_sum_b, x], axis=1) @ Wb.T + bb)
        h = x @ W_sa
        Hd = h.shape[1]
        s_left = h @ a_sa[0, :Hd]
        s_right = h @ a_sa[0, Hd:]
        scores = s_left[:, None] + s_right[None, :]
        e = jnp.where(adj_a != 0, jnp.exp(-jax.nn.leaky_relu(scores, 0.01)), 0.0)
        attn = e / (jnp.sum(e, axis=1, keepdims=True) + 1e-05)
        x_a = attn @ h
        x_b = adj_b @ (x @ W_gcnb) + b_gcnb
        return jax.nn.sigmoid(attn_a * x_a + attn_b * x_b)

    def _L1_gnn_ref(H, adj, W, b):
        import jax, jax.numpy as jnp
        import numpy as np
        N = 4096
        D_IN = 256
        HEADS = 8
        DPH = 256 // HEADS
        EDGE_P = 0.01
        H_ = jnp.einsum('nd,hde->hne', H, W)
        out = jnp.einsum('nm,hme->hne', adj, H_) + b[:, None, :]
        return jnp.transpose(out, (1, 0, 2)).reshape(H.shape[0], HEADS * DPH)

    def _L2_gnn_ref(input, adj, W, b):
        import jax, jax.numpy as jnp
        import numpy as np
        N = 4096
        IN_F = 256
        OUT_F = 256
        h = jnp.einsum('ni,oi->no', input, W) + b
        return adj @ h

    def _L3_gnn_ref(x, adj, W, b):
        import jax, jax.numpy as jnp
        import numpy as np
        EPS = 1e-08
        deg = adj.sum(axis=1)
        dis = (deg + EPS) ** (-0.5)
        a_norm = dis[:, None] * adj * dis[None, :]
        h = a_norm @ x
        return h @ W.T + b
    x = _layernorm(x + _L0_gnn_ref(x, adj, adj, L0_gnn_W_sa, L0_gnn_a_sa, L0_gnn_W_gcnb, L0_gnn_b_gcnb, L0_gnn_Wa, L0_gnn_ba, L0_gnn_Wb, L0_gnn_bb), axis=-1)
    x = _layernorm(x + _L1_gnn_ref(x, adj, L1_gnn_W, L1_gnn_b), axis=-1)
    x = _layernorm(x + _L2_gnn_ref(x, adj, L2_gnn_W, L2_gnn_b), axis=-1)
    x = _layernorm(x + _L3_gnn_ref(x, adj, L3_gnn_W, L3_gnn_b), axis=-1)
    return x

_drawn_inputs = setup_inputs


def setup_inputs(seed=0):
    import zlib

    import numpy as np

    out = dict(_drawn_inputs(seed))
    spreads = {'L1_gnn_b': (0.0, 0.1)}
    factors = {'L0_gnn_b_gcnb': 4.246, 'L2_gnn_b': 4.111, 'L3_gnn_b': 8.0}
    for name, (base, spread) in spreads.items():
        noise = np.random.default_rng([zlib.crc32(name.encode()), seed]).standard_normal(out[name].shape)
        drawn = base * np.exp(spread * noise) if base else spread * noise
        out[name] = jnp.asarray(drawn.astype(out[name].dtype))
    for name, factor in factors.items():
        out[name] = (out[name] * factor).astype(out[name].dtype)
    return out
```

```python
from contextlib import ExitStack

import concourse.bass as bass
from concourse import mybir

F32 = mybir.dt.float32
F16 = mybir.dt.float16
ALU = mybir.AluOpType
ACT = mybir.ActivationFunctionType

P = 128
CI = 512
LN_EPS = 1e-5
DEN_EPS = 1e-5
DEG_EPS = 1e-8
SLOPE = 0.01


def build(nc, x, adj, W_sa, a_sa, W_gcnb, b_gcnb, Wa, ba, Wb, bb, W1, b1, W2, b2, W3, b3, out):
    N, D = x.shape
    T = N // P
    K = D // P
    C = N // CI
    TC = CI // P
    Q = T // TC
    HEADS, _, DPH = W1.shape
    LAYERS = 3
    STEPS = LAYERS * C
    HI, LO = 0, 1
    U, ONE, V = D, D + 2, D + 2
    GW = D + 4

    with ExitStack() as ctx:
        def sb(name, shape, dt=F32):
            return ctx.enter_context(nc.sbuf_tensor(name, shape, dt))

        def sem(name):
            return ctx.enter_context(nc.semaphore(name))

        adjT = sb("adjT", [P, C, T, CI], F16)
        rows = sb("rows", [P, TC * N])
        adj_in = rows[:, :].rearrange("p (s n) -> p s n", s=TC)
        xs = rows[:, :].bitcast(F16).rearrange("p (l h t d) -> p l h t d", l=2, h=2, t=T)
        x_in = sb("x_in", [P, TC, D])
        y = x_in
        xT = sb("xT", [P, K, TC, P])
        x32 = sb("x32", [P, T, D])
        h1 = sb("h1", [P, T, D + 2])
        gs = sb("gs", [P, 2, T, GW], F16)
        sl = sb("sl", [P, 2, N])
        YT = sl[:, 0, 0:K * CI].rearrange("p (k n) -> p k n", k=K)
        lr = sb("lr", [P, TC, CI])
        er = sb("er", [P, TC, CI])
        w_raw = lr[:, 0:2, :].rearrange("p l (k n) -> p l k n", k=K)
        a_bc = er[:, 0, :]
        products = er[:, 1:3, :].rearrange("p a (k d) -> p (a k) d", d=D)
        wH = sb("wH", [P, K, D + 1])
        wG = sb("wG", [P, K, GW])
        wL = sb("wL", [P, LAYERS, K, D])
        wl = sb("wl", [P, K])
        wl_rep = sb("wl_rep", [P, K, P])
        bias = sb("bias", [P, 1 + LAYERS, D])
        bab = sb("bab", [P, 2])
        ident = sb("ident", [P, P])
        srs = sb("srs", [P, 2, T])
        vab = sb("vab", [P, T, 2])
        scale = sb("scale", [P, LAYERS, T])
        bscale = sb("bscale", [P, LAYERS, T])
        btmp = sb("btmp", [P, D])
        ab = sb("ab", [P, TC, 2])
        rd = sb("rd", [P, TC])
        v = sb("v", [P, TC, D])
        st = sb("st", [P, TC, 6])
        mv = sb("mv", [P, TC, 2])
        rs = sb("rs", [P, TC])
        half = sb("half", [P, D])
        minus_half = sb("minus_half", [P, T])

        ps = ctx.enter_context(nc.psum_tensor("ps", [P, 8, CI], F32))
        H_BANK, G_BANK, X_BANK, S_BANK = 4, 5, 6, 7
        XA = TC
        Z_BANK = 4

        x_loaded = [sem(f"x_loaded{i}") for i in range(TC)]
        adj_loaded = [sem(f"adj_loaded{i}") for i in range(TC)]
        early_weights = sem("early_weights")
        late_weights = sem("late_weights")
        ident_ready = sem("ident_ready")
        tables_ready = sem("tables_ready")
        folded = sem("folded")
        w_transposed = sem("w_transposed")
        w_copied = sem("w_copied")
        x_transposed = sem("x_transposed")
        xT_copied = sem("xT_copied")
        x_kept = sem("x_kept")
        adj_transposed = sem("adj_transposed")
        act_copied = sem("act_copied")
        dve_copied = sem("dve_copied")
        hg_done = sem("hg_done")
        hg_copied = sem("hg_copied")
        g_split = sem("g_split")
        sl_done = sem("sl_done")
        sl_copied = sem("sl_copied")
        xb_done = sem("xb_done")
        xb_read = sem("xb_read")
        lr_ready = sem("lr_ready")
        exp_done = sem("exp_done")
        e_ready = sem("e_ready")
        e_used = sem("e_used")
        ab_ready = sem("ab_ready")
        ab_tanh = sem("ab_tanh")
        sum_ready = sem("sum_ready")
        sum_tanh = sem("sum_tanh")
        xn_ready = sem("xn_ready")
        hi_ready = sem("hi_ready")
        split_ready = sem("split_ready")
        var_ready = sem("var_ready")
        rs_ready = sem("rs_ready")
        dis_ready = sem("dis_ready")
        bias_temp = sem("bias_temp")
        bias_added = sem("bias_added")
        yt_done = sem("yt_done")
        yt_copied = sem("yt_copied")
        z_done = sem("z_done")
        dve_done = sem("dve_done")
        stored = sem("stored")

        x_t = x.rearrange("(t p) d -> t p d", p=P)
        adj_t = adj.rearrange("(t p) n -> t p n", p=P)
        out_c = out.rearrange("(c t p) d -> c p t d", p=P, t=TC)
        EARLY, LATE = 3 + 4 + 3, 2 + K + 3

        def split_step(s, layers=LAYERS):
            layer = s // C
            if not isinstance(layer, int):
                layer = layer.with_bounds(min_val=0, max_val=layers - 1)
            return layer, s % C

        def row(v1):
            return v1.rearrange("(a n) -> a n", a=1)

        block = ctx.enter_context(nc.Block())

        @block.sync
        def _(sp):
            def load(c, it):
                sp.dma_start(x_in[:, it, :], x_t[c * TC + it]).then_inc(x_loaded[it], 16)

            def load_adj(c, it):
                sp.dma_start(adj_in[:, it, :], adj_t[c * TC + it]).then_inc(adj_loaded[it], 16)

            for it in range(TC):
                load(0, it)
                load_adj(0, it)
            with sp.Fori(1, C) as c:
                for it in range(TC):
                    t = c * TC + it
                    sp.wait_ge(x_transposed, t - TC + 1)
                    sp.wait_ge(x_kept, t - TC + 1)
                    load(c, it)
                    sp.wait_ge(adj_transposed, Q * (t - TC + 1))
                    load_adj(c, it)
            for c in range(C):
                sp.wait_ge(xn_ready, LAYERS * T + (c + 1) * TC)
                sp.dma_start(out_c[c], x32[:, c * TC:(c + 1) * TC, :]).then_inc(stored, 16)
            sp.wait_ge(stored, 16 * C)

        @block.gpsimd
        def _(pool):
            for l, w in ((1, W2), (2, W3)):
                pool.dma_start(w_raw[:, l - 1], w.rearrange("(k p) i -> p k i", p=P)).then_inc(late_weights, 16)
            for k in range(K):
                pool.dma_start(wL[:, 0, k, :].rearrange("p (h e) -> p h e", h=HEADS),
                               W1[:, k * P:(k + 1) * P, :].rearrange("h p e -> p h e")).then_inc(late_weights, 16)
            for n, b in enumerate((b1.rearrange("h e -> (h e)"), b2, b3)):
                pool.dma_start(bias[:, n + 1, :], row(b).broadcast_to([P, D])).then_inc(late_weights, 16)
            nc.gpsimd.memset(ident[:, :], 0.0).then_inc(ident_ready, 1)
            pool.wait_ge(ident_ready, 1)
            nc.gpsimd.affine_select(out=ident[:, :], in_=ident[:, :], compare_op=ALU.not_equal, fill=1.0,
                                    base=0, pattern=[[-1, P]], channel_multiplier=1).then_inc(ident_ready, 1)
            nc.gpsimd.memset(h1[:, :, D:D + 1], 1.0)
            nc.gpsimd.memset(gs[:, HI, :, ONE:ONE + 1], 1.0)
            nc.gpsimd.memset(gs[:, HI, :, ONE + 1:GW], 0.0)
            nc.gpsimd.memset(gs[:, LO, :, ONE:GW], 0.0)
            nc.gpsimd.memset(half[:, :], 0.5)
            nc.gpsimd.memset(minus_half[:, :], -0.5)
            nc.gpsimd.memset(scale[:, 0:2, :], 1.0)
            nc.gpsimd.memset(bscale[:, 0:1, :], 1.0)
            nc.gpsimd.memset(bscale[:, 2:3, :], 1.0).then_inc(tables_ready, 1)
            pool.wait_ge(tables_ready, 1)
            with pool.Fori(0, C) as c:
                for it in range(TC):
                    pool.wait_ge(x_loaded[it], 16 * (c + 1))
                    nc.gpsimd.tensor_tensor(x32[:, bass.ds(c * TC + it, 1), :], x_in[:, it:it + 1, :],
                                            half[:, :].rearrange("p (o d) -> p o d", o=1), ALU.add).then_inc(x_kept, 1)
            pool.wait_ge(late_weights, 16 * LATE)

            pool.sem_inc(bias_added, 1)

            def inverse_root(count, a, b):
                pool.wait_ge(var_ready, count)
                nc.gpsimd.tensor_tensor(rs[:, a:b], rs[:, a:b], minus_half[:, a:b], ALU.pow).then_inc(rs_ready, 1)

            def add_bias(n, l, t):
                pool.wait_ge(split_ready, n + 1)
                pool.wait_ge(bias_added, n + 1)
                nc.gpsimd.tensor_tensor(btmp[:, :], bias[:, bass.ds(l + 1, 1), :],
                                        bscale[:, bass.ds(l, 1), bass.ds(t, 1)].broadcast_to([P, 1, D]),
                                        ALU.mult).then_inc(bias_temp, 1)
                pool.wait_ge(bias_temp, n + 1)
                nc.gpsimd.tensor_tensor(x32[:, bass.ds(t, 1), :], x32[:, bass.ds(t, 1), :], btmp[:, :],
                                        ALU.add).then_inc(bias_added, 1)

            with pool.Fori(0, C) as c:
                inverse_root(c + 1, 0, TC)
                for it in range(TC):
                    add_bias(c * TC + it, 0, c * TC + it)
            nc.gpsimd.tensor_tensor(scale[:, 2, :], scale[:, 2, :], minus_half[:, :], ALU.pow
                                    ).then_inc(dis_ready, 1)
            with pool.Fori(0, STEPS - C) as s:
                l, c = split_step(s, LAYERS - 1)
                for pair in range(TC // 2):
                    inverse_root(C + 2 * s + pair + 1, 2 * pair, 2 * pair + 2)
                    for it in (2 * pair, 2 * pair + 1):
                        add_bias(T + s * TC + it, l + 1, c * TC + it)
            with pool.Fori(STEPS - C, STEPS) as s:
                for pair in range(TC // 2):
                    inverse_root(C + 2 * s + pair + 1, 2 * pair, 2 * pair + 2)

        @block.scalar
        def _(act):
            act.dma_start(wH[:, :, 0:D], W_sa.rearrange("(k p) e -> p k e", p=P)).then_inc(early_weights, 16)
            act.dma_start(a_bc, a_sa.broadcast_to([P, 2 * D])).then_inc(early_weights, 16)
            act.dma_start(wG[:, :, 0:D], W_gcnb.rearrange("(k p) e -> p k e", p=P)).then_inc(early_weights, 16)
            for n, w in enumerate((Wa, Wb)):
                for half in range(2):
                    act.dma_start(wG[:, :, D + 2 * half + n],
                                  w[0, half * D:(half + 1) * D].rearrange("(k p) -> p k", p=P),
                                  allow_slow_non_contiguous=True).then_inc(early_weights, 16)
            for n, b in enumerate((ba, bb)):
                act.dma_start(bab[:, n:n + 1], row(b).broadcast_to([P, 1])).then_inc(early_weights, 16)
            act.dma_start(bias[:, 0, :], row(b_gcnb).broadcast_to([P, D])).then_inc(early_weights, 16)
            act.sem_inc(xT_copied, 1)
            act.sem_inc(act_copied, 2)
            act.sem_inc(hg_copied, 1)
            act.sem_inc(sl_copied, 1)
            for l in range(1, LAYERS):
                act.wait_ge(w_transposed, l)
                nc.scalar.activation(wL[:, l, :, :].rearrange("p k n -> p (k n)"), ps[:, l - 1, :],
                                     ACT.Copy).then_inc(w_copied, 1)
            with act.Fori(0, C) as c:
                for it in range(TC):
                    t = c * TC + it
                    act.wait_ge(x_transposed, t + 1)
                    nc.scalar.activation(xT[:, :, it, :], ps[:, X_BANK, 0:D].rearrange("p (k n) -> p k n", k=K),
                                         ACT.Copy).then_inc(xT_copied, 1)
                    for q in range(2):
                        act.wait_ge(adj_transposed, Q * t + q + 1)
                        nc.scalar.activation(adjT[:, bass.ds(c, 1), TC * q:TC * (q + 1), it * P:(it + 1) * P],
                                             ps[:, q, :].rearrange("p (r n) -> p r n", r=TC),
                                             ACT.Copy).then_inc(act_copied, 1)
                    act.wait_ge(hg_done, 2 * t + 1)
                    nc.scalar.activation(h1[:, bass.ds(t, 1), 0:D], ps[:, H_BANK, 0:D], ACT.Copy)
                    act.wait_ge(hg_done, 2 * t + 2)
                    nc.scalar.activation(gs[:, HI, bass.ds(t, 1), 0:U + 2], ps[:, G_BANK, 0:U + 2],
                                         ACT.Copy).then_inc(hg_copied, 1)
                act.wait_ge(sl_done, c + 1)
                nc.scalar.activation(sl[:, 0, bass.ds(c * CI, CI)], ps[:, S_BANK, :], ACT.Copy)
                nc.scalar.activation(sl[:, 1, bass.ds(c * CI, CI)], ps[:, S_BANK, :], ACT.Copy,
                                     scale=SLOPE).then_inc(sl_copied, 1)

            with act.Fori(0, C) as c:
                for jt in range(T):
                    act.wait_ge(lr_ready, c * T + jt + 1)
                    nc.scalar.activation(lr[:, jt % TC, :], lr[:, jt % TC, :], ACT.Exp,
                                         bias=srs[:, 1, jt:jt + 1], scale=-1.0).then_inc(exp_done, 1)
                    if jt == TC:
                        act.wait_ge(ab_ready, c + 1)
                        nc.scalar.activation(ab[:, :, :], ab[:, :, :], ACT.Tanh, scale=0.5).then_inc(ab_tanh, 1)
                for it in range(TC):
                    act.wait_ge(sum_ready, c * TC + it + 2)
                    nc.scalar.activation(y[:, it, :], y[:, it, :], ACT.Tanh, scale=0.5).then_inc(sum_tanh, 1)
                for it in range(TC):
                    t = c * TC + it
                    act.wait_ge(xn_ready, t + 1)
                    nc.scalar.activation(xs[:, 0, HI, bass.ds(t, 1), :], x32[:, bass.ds(t, 1), :],
                                         ACT.Copy).then_inc(hi_ready, 1)

            def evacuate(s):
                for k in range(K):
                    act.wait_ge(yt_done, K * s + k + 1)
                    nc.scalar.activation(YT[:, k, :], ps[:, bass.ds((s % 2) * K + k, 1), :],
                                         ACT.Copy).then_inc(yt_copied, 1)

            def split_hi(s):
                l, c = split_step(s, LAYERS - 1)
                for it in range(TC):
                    act.wait_ge(xn_ready, T + s * TC + it + 1)
                    nc.scalar.activation(xs[:, bass.ds((l + 1) % 2, 1), HI,
                                            bass.ds(c * TC + it, 1), :],
                                         x32[:, bass.ds(c * TC + it, 1), :], ACT.Copy,
                                         scale=scale[:, bass.ds(l + 1, 1), bass.ds(c * TC + it, 1)]
                                         ).then_inc(hi_ready, 1)

            evacuate(0)
            act.wait_ge(dis_ready, 1)
            with act.Fori(1, STEPS - C + 1) as s:
                split_hi(s - 1)
                evacuate(s)
            with act.Fori(STEPS - C + 1, STEPS) as s:
                evacuate(s)

        @block.vector
        def _(dve):
            done = [0]

            class Chain:
                def __init__(self, turn=0, per=0):
                    self.base, self.per, self.k, self.turn = done[0], per, 0, turn

                def __call__(self, ins):
                    self.k += 1
                    ins.then_inc(dve_done, 1)

                def wait(self):
                    dve.wait_ge(dve_done, self.turn * self.per + (self.base + self.k))

                def end(self, turns=1):
                    assert turns == 1 or self.k == self.per, self.k
                    done[0] = self.base + self.k * turns

            dve.sem_inc(dve_copied, 2)
            dve.sem_inc(e_ready, TC)
            dve.sem_inc(g_split, 1)
            dve.sem_inc(xb_read, 1)
            dve.sem_inc(sum_ready, 1)
            dve.wait_ge(early_weights, 16 * EARLY)
            chain = Chain()
            for k in range(K):
                nc.vector.tensor_tensor_reduce(products[:, 2 * k, :], wH[:, k, 0:D], a_bc[:, D:2 * D], 1.0, 0.0, ALU.mult, ALU.add,
                                               wH[:, k, D:D + 1])
                chain(nc.vector.tensor_tensor_reduce(products[:, 2 * k + 1, :], wH[:, k, 0:D], a_bc[:, 0:D], 1.0, 0.0, ALU.mult,
                                                     ALU.add, wl[:, k:k + 1]))
            dve.wait_ge(ident_ready, 2)
            chain.wait()
            for k in range(K):
                nc.vector.tensor_scalar(wl_rep[:, k, :], ident[:, :], 0.0, wl[:, k:k + 1], ALU.mult,
                                        ALU.add).then_inc(folded, 1)
            chain.end()
            with dve.Fori(0, C) as c:
                for it in range(TC):
                    t = c * TC + it
                    for q in range(2, 4):
                        dve.wait_ge(adj_transposed, Q * t + q + 1)
                        nc.vector.tensor_copy(adjT[:, bass.ds(c, 1), TC * q:TC * (q + 1), it * P:(it + 1) * P],
                                              ps[:, q, :].rearrange("p (r n) -> p r n", r=TC)
                                              ).then_inc(dve_copied, 1)
                    dve.wait_ge(hg_copied, t + 2)
                    nc.vector.tensor_scalar(srs[:, 0, bass.ds(t, 1)], ps[:, H_BANK, D:D + 1], 1.0 - SLOPE, None,
                                            ALU.mult)
                    nc.vector.tensor_scalar(srs[:, 1, bass.ds(t, 1)], ps[:, H_BANK, D:D + 1], -SLOPE, None,
                                            ALU.mult)
                    nc.vector.tensor_tensor(vab[:, bass.ds(t, 1), :], ps[:, G_BANK, V:V + 2], bab[:, :], ALU.add)
                    nc.vector.tensor_tensor(gs[:, LO, bass.ds(t, 1), 0:U + 2], ps[:, G_BANK, 0:U + 2],
                                            gs[:, HI, bass.ds(t, 1), 0:U + 2], ALU.subtract).then_inc(g_split, 1)

            dve.wait_ge(sl_copied, C + 1)
            dve.wait_ge(tables_ready, 1)
            dve.wait_ge(late_weights, 16 * LATE)
            dve.wait_ge(w_copied, LAYERS - 1)
            dve.wait_ge(g_split, T + 1)
            dve.wait_ge(x_kept, T)
            with dve.Fori(0, C) as c:
                chain = Chain(c, 8)

                def leaky(jt):
                    dve.wait_ge(e_ready, c * T + jt + 1)
                    nc.vector.scalar_tensor_tensor(
                        out=lr[:, jt % TC, :], in0=sl[:, 0, bass.ds(c * CI, CI)], scalar=srs[:, 0, jt:jt + 1],
                        in1=sl[:, 1, bass.ds(c * CI, CI)], op0=ALU.add, op1=ALU.max).then_inc(lr_ready, 1)

                def mask(jt):
                    dve.wait_ge(exp_done, c * T + jt + 1)
                    dve.wait_ge(e_used, c * T + jt + 1)
                    nc.vector.tensor_tensor(er[:, jt % TC, :], lr[:, jt % TC, :], adjT[:, bass.ds(c, 1), jt, :],
                                            ALU.mult).then_inc(e_ready, 1)

                leaky(0)
                leaky(1)
                for jt in range(T):
                    if jt + 2 < T:
                        leaky(jt + 2)
                    mask(jt)
                    if jt == TC - 1:
                        dve.wait_ge(xb_done, c + 1)
                        nc.vector.tensor_tensor(ab[:, :, :], ps[:, 0:TC, U:U + 2], vab[:, bass.ds(c * TC, TC), :],
                                                ALU.add).then_inc(ab_ready, 1)
                        nc.vector.tensor_copy(bscale[:, 1, bass.ds(c * TC, TC)], ps[:, 0:TC, ONE])
                        nc.vector.tensor_scalar(scale[:, 2, bass.ds(c * TC, TC)], ps[:, 0:TC, ONE], DEG_EPS, None,
                                                ALU.add)
                        for it in range(TC):
                            ins = nc.vector.tensor_tensor(y[:, it, :], ps[:, it, 0:D], bias[:, 0, :], ALU.add)
                            if it == TC - 1:
                                ins.then_inc(xb_read, 1)
                    if jt == TC + 2:
                        dve.wait_ge(ab_tanh, c + 1)
                        chain(nc.vector.tensor_scalar(ab[:, :, :], ab[:, :, :], 0.5, 0.5, ALU.mult, ALU.add))
                        chain.wait()
                        dve.wait_ge(xb_read, c + 2)
                        for it in range(TC):
                            ins = nc.vector.tensor_scalar(y[:, it, :], y[:, it, :], ab[:, it, 1:2], None, ALU.mult)
                        chain(ins)
                dve.wait_ge(e_used, (c + 1) * T + TC)
                chain(nc.vector.tensor_scalar(rd[:, :], ps[:, XA:XA + TC, D], DEN_EPS, None, ALU.add))
                chain.wait()
                chain(nc.vector.reciprocal(rd[:, :], rd[:, :]))
                chain.wait()
                chain(nc.vector.tensor_tensor(rd[:, :], rd[:, :], ab[:, :, 0], ALU.mult))
                chain.wait()
                for it in range(TC):
                    ins = nc.vector.scalar_tensor_tensor(out=y[:, it, :], in0=ps[:, XA + it, 0:D],
                                                         scalar=rd[:, it:it + 1], in1=y[:, it, :],
                                                         op0=ALU.mult, op1=ALU.add)
                    ins.then_inc(sum_ready, 1)
                for it in range(TC):
                    dve.wait_ge(sum_tanh, c * TC + it + 1)
                    ins = nc.vector.scalar_tensor_tensor(out=y[:, it, :], in0=y[:, it, :], scalar=0.5,
                                                         in1=x32[:, bass.ds(c * TC + it, 1), :],
                                                         op0=ALU.mult, op1=ALU.add)
                chain(ins)
                chain.wait()
                for it in range(TC):
                    ins = nc.vector.bn_stats(st[:, it, :], y[:, it, :])
                chain(ins)
                chain.wait()
                dve.nop(nofuse=True)
                for it in range(TC):
                    ins = nc.vector.bn_aggr(mv[:, it, :], st[:, it, :])
                chain(ins)
                chain.wait()
                nc.vector.tensor_scalar(rs[:, :], mv[:, :, 1], LN_EPS, None, ALU.add).then_inc(var_ready, 1)
                dve.wait_ge(rs_ready, c + 1)
                for it in range(TC):
                    nc.vector.tensor_scalar(x32[:, bass.ds(c * TC + it, 1), :], y[:, it, :], mv[:, it, 0:1],
                                            rs[:, it:it + 1], ALU.subtract, ALU.mult).then_inc(xn_ready, 1)
                for it in range(TC):
                    t = c * TC + it
                    dve.wait_ge(hi_ready, t + 1)
                    ins = nc.vector.tensor_tensor(xs[:, 0, LO, bass.ds(t, 1), :], x32[:, bass.ds(t, 1), :],
                                                  xs[:, 0, HI, bass.ds(t, 1), :], ALU.subtract)
                    ins.then_inc(split_ready, 1)
            chain.end(C)

            dve.wait_ge(dis_ready, 1)

            def norm(s, chain, last):
                l, c = split_step(s, LAYERS if last else LAYERS - 1)
                for pair in range(TC // 2):
                    for i in range(2):
                        it = 2 * pair + i
                        dve.wait_ge(z_done, s * TC + it + 1)
                        dve.wait_ge(bias_added, s * TC + it + 2)
                        ins = nc.vector.scalar_tensor_tensor(
                            out=v[:, it, :], in0=ps[:, Z_BANK + it, 0:D],
                            scalar=scale[:, bass.ds(l, 1), bass.ds(c * TC + it, 1)],
                            in1=x32[:, bass.ds(c * TC + it, 1), :], op0=ALU.mult, op1=ALU.add)
                    chain(ins)
                    chain.wait()
                    for i in range(2):
                        ins = nc.vector.bn_stats(st[:, 2 * pair + i, :], v[:, 2 * pair + i, :])
                    chain(ins)
                    chain.wait()
                    dve.nop(nofuse=True)
                    for i in range(2):
                        ins = nc.vector.bn_aggr(mv[:, 2 * pair + i, :], st[:, 2 * pair + i, :])
                    chain(ins)
                    chain.wait()
                    nc.vector.tensor_scalar(rs[:, 2 * pair:2 * pair + 2], mv[:, 2 * pair:2 * pair + 2, 1], LN_EPS, None,
                                            ALU.add).then_inc(var_ready, 1)
                    dve.wait_ge(rs_ready, C + 2 * s + pair + 1)
                    for i in range(2):
                        it = 2 * pair + i
                        nc.vector.tensor_scalar(x32[:, bass.ds(c * TC + it, 1), :], v[:, it, :], mv[:, it, 0:1],
                                                rs[:, it:it + 1], ALU.subtract, ALU.mult).then_inc(xn_ready, 1)
                    if last:
                        continue
                    for i in range(2):
                        it = 2 * pair + i
                        t = c * TC + it
                        dve.wait_ge(hi_ready, T + s * TC + it + 1)
                        nc.vector.scalar_tensor_tensor(
                            out=xs[:, bass.ds((l + 1) % 2, 1), LO, bass.ds(t, 1), :],
                            in0=x32[:, bass.ds(t, 1), :], scalar=scale[:, bass.ds(l + 1, 1), bass.ds(t, 1)],
                            in1=xs[:, bass.ds((l + 1) % 2, 1), HI, bass.ds(t, 1), :],
                            op0=ALU.mult, op1=ALU.subtract).then_inc(split_ready, 1)

            with dve.Fori(0, STEPS - C) as s:
                chain = Chain(s, 6)
                norm(s, chain, False)
            chain.end(STEPS - C)
            with dve.Fori(STEPS - C, STEPS) as s:
                chain = Chain(s - (STEPS - C), 6)
                norm(s, chain, True)

        @block.tensor
        def _(pe):
            pe.sem_inc(e_used, TC)
            pe.wait_ge(ident_ready, 2)
            pe.wait_ge(late_weights, 16 * LATE)
            for l in range(1, LAYERS):
                for ki in range(K):
                    for ko in range(K):
                        ins = pe.transpose(ps[:, l - 1, (ki * K + ko) * P:(ki * K + ko + 1) * P],
                                           w_raw[:, l - 1, ko, ki * P:(ki + 1) * P], ident[:, :])
                ins.then_inc(w_transposed, 1)
            pe.wait_ge(w_copied, LAYERS - 1)
            pe.wait_ge(folded, K)
            with pe.Fori(0, C) as c:
                for it in range(TC):
                    t = c * TC + it
                    pe.wait_ge(x_loaded[it], 16 * (c + 1))
                    pe.wait_ge(xT_copied, t + 1)
                    for k in range(K):
                        ins = pe.transpose(ps[:, X_BANK, k * P:(k + 1) * P], x_in[:, it, k * P:(k + 1) * P],
                                           ident[:, :])
                    ins.then_inc(x_transposed, 1)
                    pe.wait_ge(adj_loaded[it], 16 * (c + 1))
                    for q in range(Q):
                        pe.wait_ge(act_copied if q < 2 else dve_copied, 2 * t + q % 2 + 1)
                        for r in range(TC):
                            jt = q * TC + r
                            ins = pe.transpose(ps[:, q, r * P:(r + 1) * P], adj_in[:, it, jt * P:(jt + 1) * P],
                                               ident[:, :])
                        ins.then_inc(adj_transposed, 1)
                    pe.wait_ge(xT_copied, t + 2)
                    pe.wait_ge(hg_copied, t + 1)
                    pe.wait_ge(g_split, t + 1)
                    for bank, w, width in ((H_BANK, wH, D + 1), (G_BANK, wG, GW)):
                        for k in range(K):
                            ins = pe.matmul(ps[:, bank, 0:width], xT[:, k, it, :], w[:, k, :], start=(k == 0),
                                            stop=(k == K - 1))
                        ins.then_inc(hg_done, 1)
                pe.wait_ge(sl_copied, c + 1)
                for k in range(K):
                    ins = pe.matmul(ps[:, S_BANK, :], wl_rep[:, k, :], xT[:, k, :, :], start=(k == 0),
                                    stop=(k == K - 1))
                ins.then_inc(sl_done, 1)

            pe.wait_ge(act_copied, 2 * T + 2)
            pe.wait_ge(dve_copied, 2 * T + 2)
            pe.wait_ge(hg_copied, T + 1)
            pe.wait_ge(g_split, T + 1)
            pe.wait_ge(sl_copied, C + 1)
            pe.wait_ge(tables_ready, 1)
            with pe.Fori(0, C) as c:
                pe.wait_ge(xb_read, c + 1)
                for jt in range(T):
                    for it in range(TC):
                        for part in (HI, LO):
                            ins = pe.matmul(ps[:, it, 0:GW], adjT[:, bass.ds(c, 1), jt, it * P:(it + 1) * P],
                                            gs[:, part, jt, :], start=(jt == 0 and part == HI),
                                            stop=(jt == T - 1 and part == LO))
                ins.then_inc(xb_done, 1)
                pe.wait_ge(sum_ready, c * TC + 1)
                for jt in range(T):
                    pe.wait_ge(e_ready, c * T + jt + TC + 1)
                    for it in range(TC):
                        ins = pe.matmul(ps[:, XA + it, 0:D + 1], er[:, jt % TC, it * P:(it + 1) * P],
                                        h1[:, jt, 0:D + 1], start=(jt == 0), stop=(jt == T - 1))
                    ins.then_inc(e_used, 1)

            def aggregate(s, k, tiles):
                l, c = split_step(s)
                for jt in tiles:
                    for part in (HI, LO):
                        ins = pe.matmul(ps[:, bass.ds((s % 2) * K + k, 1), :],
                                        xs[:, bass.ds(l % 2, 1), part, jt, k * P:(k + 1) * P],
                                        adjT[:, bass.ds(c, 1), jt, :],
                                        start=(jt == 0 and part == HI), stop=(jt == T - 1 and part == LO))
                return ins

            def project(s):
                pe.wait_ge(yt_copied, K * (s + 1))
                pe.wait_ge(var_ready, C + 2 * s)
                for it in range(TC):
                    for k in range(K):
                        ins = pe.matmul(ps[:, Z_BANK + it, 0:D],
                                        YT[:, k, it * P:(it + 1) * P], wL[:, bass.ds(split_step(s)[0], 1), k, :],
                                        start=(k == 0), stop=(k == K - 1))
                    ins.then_inc(z_done, 1)

            FIRST, REST = range(T - TC), range(T - TC, T)

            def step(s, project_last):
                pe.wait_ge(split_ready, split_step(s)[0] * T + (T - TC))
                aggregate(s, 0, FIRST)
                if project_last:
                    project(s - 1)
                aggregate(s, 1, FIRST)
                pe.wait_ge(split_ready, split_step(s)[0] * T + T)
                for k in range(K):
                    aggregate(s, k, REST).then_inc(yt_done, 1)

            step(0, False)
            with pe.Fori(1, STEPS) as s:
                step(s, True)
            project(STEPS - 1)


_INS = ['x', 'adj', 'L0_gnn_W_sa', 'L0_gnn_a_sa', 'L0_gnn_W_gcnb', 'L0_gnn_b_gcnb', 'L0_gnn_Wa', 'L0_gnn_ba',
        'L0_gnn_Wb', 'L0_gnn_bb', 'L1_gnn_W', 'L1_gnn_b', 'L2_gnn_W', 'L2_gnn_b', 'L3_gnn_W', 'L3_gnn_b']


def kernel(**inputs):
    import numpy as _np
    import concourse.bacc as _bacc
    from concourse import mybir as _mybir
    from concourse.bass_utils import run_bass_kernel_spmd as _run

    nc = _bacc.Bacc("TRN2", target_bir_lowering=False, num_devices=1)
    arrays, args = {}, []
    for name in _INS:
        a = _np.ascontiguousarray(inputs[name])
        arrays[f"in_{name}_dram"] = a
        args.append(nc.dram_tensor(f"in_{name}_dram", a.shape, _mybir.dt.from_np(a.dtype), kind="ExternalInput").ap())
    shape = inputs['x'].shape
    args.append(nc.dram_tensor("out_0_dram", shape, _mybir.dt.float32, kind="ExternalOutput").ap())
    build(nc, *args)
    r = _run(nc, [arrays], core_ids=[0])
    return r.results[0]["out_0_dram"]
```

```python
import math
from contextlib import ExitStack

import concourse.bass as bass
from concourse import mybir

F32 = mybir.dt.float32
F16 = mybir.dt.float16
ALU = mybir.AluOpType
ACT = mybir.ActivationFunctionType

P = 128
CI = 512
LN_EPS = 1e-5
DEN_EPS = 1e-5
DEG_EPS = 1e-8
SLOPE = 0.01
E_EXP = 15
W_EXP = 6
HI, LO = 0, 1
PARTS = ((HI, HI), (HI, LO), (LO, HI))


def build(nc, x, adj, W_sa, a_sa, W_gcnb, b_gcnb, Wa, ba, Wb, bb, W1, b1, W2, b2, W3, b3, out):
    N, D = x.shape
    T = N // P
    K = D // P
    C = N // CI
    TC = CI // P
    HALF = T // 2
    RING = 2 * TC
    HEADS = W1.shape[0]
    LAYERS = 3
    STEPS = LAYERS * C
    HW = D + 2
    U, ONE, V = D, D + 2, D + 2
    GW = D + 4

    with ExitStack() as ctx:
        def sb(name, shape, dt=F32):
            return ctx.enter_context(nc.sbuf_tensor(name, shape, dt))

        def sem(name):
            return ctx.enter_context(nc.semaphore(name))

        adjT = sb("adjT", [P, C, T, CI], F16)
        rows = sb("rows", [P, TC * N])
        adj_in = rows[:, :].rearrange("p (s n) -> p s n", s=TC)
        xs = rows[:, :].bitcast(F16).rearrange("p (l h t d) -> p l h t d", l=2, h=2, t=T)
        x_in = sb("x_in", [P, TC, D])
        y = x_in
        xT = sb("xT", [P, K, TC, P])
        x32 = sb("x32", [P, T, D])
        hs = sb("hs", [P, 2, T, HW], F16)
        gs = sb("gs", [P, 2, T, GW], F16)
        sl = sb("sl", [P, N])
        YT = sl[:, 0:K * CI].bitcast(F16).rearrange("p (h k n) -> p h k n", h=2, k=K)
        products = sl[:, 0:2 * K * D].rearrange("p (k d) -> p k d", d=D)
        lr = sb("lr", [P, TC, CI])
        er = sb("er", [P, RING, 2, CI], F16)
        adj16 = er[:, 0:TC, :, :].rearrange("p s h n -> p (s h n)").rearrange("p (s n) -> p s n", s=2)
        a_bc = lr[:, 2, :]
        w1_raw = lr[:, 3, :].rearrange("p (k n) -> p k n", k=K)
        wH = sb("wH", [P, K, HW])
        wG = sb("wG", [P, K, GW])
        wL = sb("wL", [P, LAYERS, 2, K, D], F16)
        bias = sb("bias", [P, 1 + LAYERS, D])
        bab = sb("bab", [P, 2])
        ident = sb("ident", [P, P])
        ident16 = sb("ident16", [P, P], F16)
        sl_col = sb("sl_col", [P, TC])
        srs = sb("srs", [P, 2, T])
        row_eps = sb("row_eps", [P, T])
        top = sb("top", [P, 2])
        vab = sb("vab", [P, T, 2])
        scale = sb("scale", [P, LAYERS, T])
        zscale = sb("zscale", [P, LAYERS, T])
        bscale = sb("bscale", [P, LAYERS, T])
        btmp = sb("btmp", [P, D])
        half = sb("half", [P, D])
        minus_half = sb("minus_half", [P, T])
        ab = sb("ab", [P, TC, 2])
        rd = sb("rd", [P, TC])
        v = sb("v", [P, TC, D])
        w_raw = v[:, :, :].rearrange("p (l k) n -> p l k n", k=K)
        st = sb("st", [P, TC, 6])
        mv = sb("mv", [P, TC, 2])
        rs = sb("rs", [P, TC])

        ps = ctx.enter_context(nc.psum_tensor("ps", [P, 8, CI], F32))
        X_BANK, S_BANK = 6, 7
        TOP_BANK = 5
        XA = TC
        Z_BANK = 4

        def blocks(part):
            return ps[:, part, :].bitcast(F16).rearrange("p (r n) -> p r n", n=P)

        def h_bank(it):
            return 2 + 2 * (it % 2)

        def g_bank(it):
            return h_bank(it) + 1

        def wt(l):
            return ps[:, X_BANK if l == 1 else h_bank(1), :].rearrange("p (k n) -> p k n", k=K)

        x_loaded = [sem(f"x_loaded{i}") for i in range(TC)]
        adj_loaded = [sem(f"adj_loaded{i}") for i in range(TC)]
        sa_weights = sem("sa_weights")
        gcn_weights = sem("gcn_weights")
        bab_loaded = sem("bab_loaded")
        square_weights = sem("square_weights")
        w1_loaded = sem("w1_loaded")
        biases_loaded = sem("biases_loaded")
        ident_ready = sem("ident_ready")
        tables_ready = sem("tables_ready")
        folded = sem("folded")
        cols_copied = sem("cols_copied")
        top_local = sem("top_local")
        top_spread = sem("top_spread")
        shifted = sem("shifted")
        w_transposed = sem("w_transposed")
        w_hi = sem("w_hi")
        w_split = sem("w_split")
        x_transposed = sem("x_transposed")
        xT_copied = sem("xT_copied")
        x_kept = sem("x_kept")
        adj_cast = sem("adj_cast")
        adj_transposed = sem("adj_transposed")
        act_copied = sem("act_copied")
        dve_copied = sem("dve_copied")
        hg_done = sem("hg_done")
        hg_copied = sem("hg_copied")
        hg_split = sem("hg_split")
        sl_done = sem("sl_done")
        sl_copied = sem("sl_copied")
        eps_ready = sem("eps_ready")
        xb_done = sem("xb_done")
        xb_read = sem("xb_read")
        relu_ready = sem("relu_ready")
        dve_relu_ready = sem("dve_relu_ready")
        exp_done = sem("exp_done")
        rest_ready = sem("rest_ready")
        e_ready = sem("e_ready")
        e_used = sem("e_used")
        ab_ready = sem("ab_ready")
        ab_tanh = sem("ab_tanh")
        sum_ready = sem("sum_ready")
        sum_tanh = sem("sum_tanh")
        xn_ready = sem("xn_ready")
        hi_ready = sem("hi_ready")
        split_ready = sem("split_ready")
        var_ready = sem("var_ready")
        rs_ready = sem("rs_ready")
        dis_ready = sem("dis_ready")
        bias_temp = sem("bias_temp")
        bias_added = sem("bias_added")
        yt_done = sem("yt_done")
        yt_hi = sem("yt_hi")
        yt_split = sem("yt_split")
        z_done = sem("z_done")
        dve_done = sem("dve_done")
        stored = sem("stored")

        x_t = x.rearrange("(t p) d -> t p d", p=P)
        adj_t = adj.rearrange("(t p) n -> t p n", p=P)
        out_p = out.rearrange("(c t p) d -> c p t d", p=P, t=2)

        def split_step(s, layers=LAYERS):
            layer = s // C
            if not isinstance(layer, int):
                layer = layer.with_bounds(min_val=0, max_val=layers - 1)
            return layer, s % C

        def row(v1):
            return v1.rearrange("(a n) -> a n", a=1)

        DVE_SLOT = 2
        ACT_RELUS = T - T // TC

        def act_relus(jt):
            return jt + 1 - (jt + TC - DVE_SLOT) // TC

        SUM_AT, TANH_AT, NORM_AT, HI_AT, LO_AT = 1, 4, 5, 9, 10
        AGG_AT, GATE_AT, GATED_AT = RING - 1, RING + 2, RING + 3

        block = ctx.enter_context(nc.Block())

        @block.sync
        def _(sp):
            def load(c, it):
                sp.dma_start(x_in[:, it, :], x_t[c * TC + it]).then_inc(x_loaded[it], 16)

            def load_adj(c, it):
                sp.dma_start(adj_in[:, it, :], adj_t[c * TC + it]).then_inc(adj_loaded[it], 16)

            load(0, 0)
            sp.dma_start(a_bc, a_sa.broadcast_to([P, 2 * D])).then_inc(sa_weights, 16)
            sp.dma_start(wG[:, :, 0:D], W_gcnb.rearrange("(k p) e -> p k e", p=P)).then_inc(gcn_weights, 16)
            load_adj(0, 0)
            for it in range(1, TC):
                load(0, it)
                load_adj(0, it)
            with sp.Fori(1, C) as c:
                for it in range(TC):
                    t = c * TC + it
                    sp.wait_ge(x_transposed, t - TC + 1)
                    sp.wait_ge(x_kept, t - TC + 1)
                    load(c, it)
                    sp.wait_ge(adj_cast, 2 * (t - TC + 1))
                    load_adj(c, it)
            for l, w in ((1, W2), (2, W3)):
                sp.dma_start(w_raw[:, l - 1], w.rearrange("(k p) i -> p k i", p=P)).then_inc(square_weights, 16)
            for t in range(0, T, 2):
                sp.wait_ge(xn_ready, LAYERS * T + t + 2)
                sp.dma_start(out_p[t // 2], x32[:, t:t + 2, :]).then_inc(stored, 16)
            sp.wait_ge(stored, 16 * (T // 2))

        @block.gpsimd
        def _(pool):
            nc.gpsimd.memset(ident[:, :], 0.0).then_inc(ident_ready, 1)
            pool.wait_ge(ident_ready, 1)
            nc.gpsimd.affine_select(out=ident[:, :], in_=ident[:, :], compare_op=ALU.not_equal, fill=1.0,
                                    base=0, pattern=[[-1, P]], channel_multiplier=1).then_inc(ident_ready, 1)
            pool.wait_ge(ident_ready, 2)
            nc.gpsimd.tensor_copy(ident16[:, :], ident[:, :]).then_inc(ident_ready, 1)
            nc.gpsimd.memset(half[:, :], 0.5)
            nc.gpsimd.memset(minus_half[:, :], -0.5)
            nc.gpsimd.memset(hs[:, HI, :, D:D + 1], 1.0)
            nc.gpsimd.memset(gs[:, HI, :, ONE:ONE + 1], 1.0)
            nc.gpsimd.memset(gs[:, HI, :, ONE + 1:GW], 0.0)
            nc.gpsimd.memset(gs[:, LO, :, ONE:GW], 0.0)
            nc.gpsimd.memset(scale[:, 0:2, :], 1.0)
            nc.gpsimd.memset(zscale[:, 0:2, :], 2.0 ** -W_EXP)
            nc.gpsimd.memset(bscale[:, 0:1, :], 1.0)
            nc.gpsimd.memset(bscale[:, 2:3, :], 1.0).then_inc(tables_ready, 1)
            pool.wait_ge(tables_ready, 1)

            def keep(c):
                for it in range(TC):
                    pool.wait_ge(x_loaded[it], 16 * (c + 1))
                    nc.gpsimd.tensor_tensor(x32[:, bass.ds(c * TC + it, 1), :], x_in[:, it:it + 1, :],
                                            half[:, :].rearrange("p (o d) -> p o d", o=1), ALU.add
                                            ).then_inc(x_kept, 1)

            with pool.Fori(0, C) as c:
                keep(c)
            for k in range(K):
                pool.dma_start(w1_raw[:, k, :].rearrange("p (h e) -> p h e", h=HEADS),
                               W1[:, k * P:(k + 1) * P, :].rearrange("h p e -> p h e")).then_inc(w1_loaded, 16)
            for n, b in enumerate((b_gcnb, b1.rearrange("h e -> (h e)"), b2, b3)):
                pool.dma_start(bias[:, n, :], row(b).broadcast_to([P, D])).then_inc(biases_loaded, 16)
            pool.wait_ge(biases_loaded, 16 * (1 + LAYERS))
            pool.sem_inc(bias_added, 1)

            def inverse_root(count, a, b):
                pool.wait_ge(var_ready, count)
                nc.gpsimd.tensor_tensor(rs[:, a:b], rs[:, a:b], minus_half[:, a:b], ALU.pow).then_inc(rs_ready, 1)

            def add_bias(n, l, t):
                pool.wait_ge(split_ready, n + 1)
                pool.wait_ge(bias_added, n + 1)
                nc.gpsimd.tensor_tensor(btmp[:, :], bias[:, bass.ds(l + 1, 1), :],
                                        bscale[:, bass.ds(l, 1), bass.ds(t, 1)].broadcast_to([P, 1, D]),
                                        ALU.mult).then_inc(bias_temp, 1)
                pool.wait_ge(bias_temp, n + 1)
                nc.gpsimd.tensor_tensor(x32[:, bass.ds(t, 1), :], x32[:, bass.ds(t, 1), :], btmp[:, :],
                                        ALU.add).then_inc(bias_added, 1)

            with pool.Fori(0, C - 1) as c:
                inverse_root(c + 1, 0, TC)
                for it in range(TC):
                    add_bias(c * TC + it, 0, c * TC + it)
            pool.wait_ge(xb_read, C + 1)
            nc.gpsimd.tensor_tensor(scale[:, 2, :], scale[:, 2, :], minus_half[:, :], ALU.pow
                                    ).then_inc(dis_ready, 1)
            inverse_root(C, 0, TC)
            for it in range(TC):
                add_bias((C - 1) * TC + it, 0, (C - 1) * TC + it)
            with pool.Fori(0, STEPS - C) as s:
                l, c = split_step(s, LAYERS - 1)
                for pair in range(TC // 2):
                    inverse_root(C + 2 * s + pair + 1, 2 * pair, 2 * pair + 2)
                for it in range(TC):
                    add_bias(T + s * TC + it, l + 1, c * TC + it)
            with pool.Fori(STEPS - C, STEPS) as s:
                for pair in range(TC // 2):
                    inverse_root(C + 2 * s + pair + 1, 2 * pair, 2 * pair + 2)

        @block.scalar
        def _(act):
            act.dma_start(wH[:, :, 0:D], W_sa.rearrange("(k p) e -> p k e", p=P)).then_inc(sa_weights, 16)
            for n, w in enumerate((Wa, Wb)):
                for part in range(2):
                    act.dma_start(wG[:, :, D + 2 * part + n],
                                  w[0, part * D:(part + 1) * D].rearrange("(k p) -> p k", p=P),
                                  allow_slow_non_contiguous=True).then_inc(gcn_weights, 16)
            for n, b in enumerate((ba, bb)):
                act.dma_start(bab[:, n:n + 1], row(b).broadcast_to([P, 1])).then_inc(bab_loaded, 16)
            act.sem_inc(xT_copied, 1)
            act.sem_inc(act_copied, 1)
            act.sem_inc(sl_copied, 1)

            def copy_x(c, it):
                act.wait_ge(x_transposed, c * TC + it + 1)
                nc.scalar.activation(xT[:, :, it, :], ps[:, X_BANK, 0:D].rearrange("p (k n) -> p k n", k=K),
                                     ACT.Copy).then_inc(xT_copied, 1)

            def take_tile(c, it, ahead):
                t = c * TC + it
                if ahead:
                    copy_x(c + (it + 1) // TC, (it + 1) % TC)
                act.wait_ge(cols_copied, t + 1)
                act.nop(nofuse=True)
                nc.scalar.activation(hs[:, HI, bass.ds(t, 1), 0:D], ps[:, h_bank(it), 0:D], ACT.Copy)
                act.wait_ge(hg_done, 2 * t + 2)
                act.nop(nofuse=True)
                nc.scalar.activation(gs[:, HI, bass.ds(t, 1), 0:U + 2], ps[:, g_bank(it), 0:U + 2],
                                     ACT.Copy).then_inc(hg_copied, 1)
                act.wait_ge(adj_transposed, 2 * t + 2)
                act.nop(nofuse=True)
                nc.scalar.activation(adjT[:, bass.ds(c, 1), HALF:T, it * P:(it + 1) * P], blocks(1),
                                     ACT.Copy).then_inc(act_copied, 1)
                if it == TC - 1:
                    act.wait_ge(sl_done, c + 2)
                    act.nop(nofuse=True)
                    nc.scalar.activation(sl[:, bass.ds(c * CI, CI)], ps[:, S_BANK, :], ACT.Copy,
                                         scale=1.0 - SLOPE).then_inc(sl_copied, 1)

            copy_x(0, 0)
            with act.Fori(0, C - 1) as c:
                for it in range(TC):
                    take_tile(c, it, True)
            for it in range(TC):
                take_tile(C - 1, it, it + 1 < TC)
            def split_weights_hi(l):
                if l == 0:
                    act.wait_ge(w1_loaded, 16 * K)
                else:
                    act.wait_ge(w_transposed, l)
                nc.scalar.activation(wL[:, l, HI, :, :], wt(l) if l else w1_raw, ACT.Copy,
                                     scale=2.0 ** W_EXP).then_inc(w_hi, 1)

            act.wait_ge(adj_transposed, 2 * T)

            def exponentials(c, tail):
                for jt in range(T):
                    n = c * T + jt
                    if jt % TC != DVE_SLOT:
                        if jt == TC - 1 and not tail:
                            act.wait_ge(w_split, 1)
                        act.wait_ge(rest_ready, n + 1)
                        act.nop(nofuse=True)
                        nc.scalar.activation(lr[:, jt % TC, :], sl[:, bass.ds(c * CI, CI)], ACT.Relu,
                                             bias=srs[:, 0, jt:jt + 1]).then_inc(relu_ready, 1)
                        act.wait_ge(relu_ready, c * ACT_RELUS + act_relus(jt))
                    else:
                        act.wait_ge(dve_relu_ready, c * (T - ACT_RELUS) + jt // TC + 1)
                    if jt == 0 and not tail:
                        act.wait_ge(shifted, 1)
                        nc.scalar.activation(row_eps[:, :], row_eps[:, :], ACT.Exp).then_inc(eps_ready, 1)
                    act.wait_ge(e_used, n + 1)
                    nc.scalar.activation(er[:, jt % RING, HI, :], lr[:, jt % TC, :], ACT.Exp,
                                         bias=srs[:, 1, jt:jt + 1], scale=-1.0)
                    nc.scalar.activation(lr[:, jt % TC, :], lr[:, jt % TC, :], ACT.Exp,
                                         bias=srs[:, 1, jt:jt + 1], scale=-1.0).then_inc(exp_done, 1)
                    if jt < LAYERS and not tail:
                        split_weights_hi(jt)
                    if jt == TANH_AT and tail:
                        squash_sum(c - 1)
                    if jt == HI_AT and tail:
                        split_hi_0(c - 1)
                    if jt == GATE_AT:
                        act.wait_ge(ab_ready, c + 1)
                        nc.scalar.activation(ab[:, :, :], ab[:, :, :], ACT.Tanh, scale=0.5).then_inc(ab_tanh, 1)

            def squash_sum(c):
                for it in range(TC):
                    act.wait_ge(sum_ready, c * TC + it + 2)
                    nc.scalar.activation(y[:, it, :], y[:, it, :], ACT.Tanh, scale=0.5).then_inc(sum_tanh, 1)

            def split_hi_0(c):
                for it in range(TC):
                    t = c * TC + it
                    act.wait_ge(xn_ready, t + 1)
                    act.nop(nofuse=True)
                    nc.scalar.activation(xs[:, 0, HI, bass.ds(t, 1), :], x32[:, bass.ds(t, 1), :],
                                         ACT.Copy).then_inc(hi_ready, 1)

            exponentials(0, False)
            with act.Fori(1, C) as c:
                exponentials(c, True)
            squash_sum(C - 1)
            split_hi_0(C - 1)

            def evacuate(s):
                for k in range(K):
                    act.wait_ge(yt_done, K * s + k + 1)
                    nc.scalar.activation(YT[:, HI, k, :], ps[:, bass.ds((s % 2) * K + k, 1), :],
                                         ACT.Copy).then_inc(yt_hi, 1)

            def split_hi(s):
                l, c = split_step(s, LAYERS - 1)
                for it in range(TC):
                    act.wait_ge(xn_ready, T + s * TC + it + 1)
                    nc.scalar.activation(xs[:, bass.ds((l + 1) % 2, 1), HI, bass.ds(c * TC + it, 1), :],
                                         x32[:, bass.ds(c * TC + it, 1), :], ACT.Copy,
                                         scale=scale[:, bass.ds(l + 1, 1), bass.ds(c * TC + it, 1)]
                                         ).then_inc(hi_ready, 1)

            evacuate(0)
            act.wait_ge(dis_ready, 1)
            with act.Fori(1, STEPS - C + 1) as s:
                split_hi(s - 1)
                evacuate(s)
            with act.Fori(STEPS - C + 1, STEPS) as s:
                evacuate(s)

        @block.vector
        def _(dve):
            done = [0]

            class Chain:
                def __init__(self, turn=0, per=0):
                    self.base, self.per, self.k, self.turn = done[0], per, 0, turn

                def __call__(self, ins):
                    self.k += 1
                    ins.then_inc(dve_done, 1)

                def wait(self, back=0):
                    dve.wait_ge(dve_done, self.turn * self.per + (self.base + self.k - back))

                def end(self, turns=1):
                    assert turns == 1 or self.k == self.per, self.k
                    done[0] = self.base + self.k * turns

            dve.sem_inc(dve_copied, 1)
            dve.sem_inc(hg_split, 2)
            dve.sem_inc(xb_read, 1)
            dve.sem_inc(sum_ready, 1)
            dve.sem_inc(rest_ready, TC)
            dve.sem_inc(sl_done, 1)
            dve.wait_ge(sa_weights, 16 * 2)
            chain = Chain()
            for k in range(K):
                for side in range(2):
                    nc.vector.tensor_tensor_reduce(
                        products[:, 2 * k + side, :], wH[:, k, 0:D], a_bc[:, (1 - side) * D:(2 - side) * D], 1.0, 0.0,
                        ALU.mult, ALU.add, wH[:, k, D + side:D + side + 1]).then_inc(folded, 1)
            chain.end()
            dve.wait_ge(bab_loaded, 16 * 2)
            with dve.Fori(0, C) as c:
                for it in range(TC):
                    t = c * TC + it
                    h, g = h_bank(it), g_bank(it)
                    dve.wait_ge(adj_loaded[it], 16 * (c + 1))
                    for part in range(2):
                        nc.vector.tensor_copy(adj16[:, it % 2, part * HALF * P:(part + 1) * HALF * P],
                                              adj_in[:, it, part * HALF * P:(part + 1) * HALF * P]
                                              ).then_inc(adj_cast, 1)
                    dve.wait_ge(hg_done, 2 * t + 1)
                    if it == 0:
                        dve.wait_ge(sl_done, c + 1)
                    nc.vector.tensor_copy(sl_col[:, it:it + 1], ps[:, h, D + 1:D + 2])
                    nc.vector.tensor_copy(row_eps[:, bass.ds(t, 1)], ps[:, h, D + 1:D + 2])
                    nc.vector.tensor_scalar(srs[:, 0, bass.ds(t, 1)], ps[:, h, D:D + 1], 1.0 - SLOPE, None, ALU.mult)
                    nc.vector.tensor_scalar(srs[:, 1, bass.ds(t, 1)], ps[:, h, D:D + 1], -SLOPE, None,
                                            ALU.mult).then_inc(cols_copied, 1)
                    dve.wait_ge(adj_transposed, 2 * t + 1)
                    nc.vector.tensor_copy(adjT[:, bass.ds(c, 1), 0:HALF, it * P:(it + 1) * P],
                                          blocks(0)).then_inc(dve_copied, 1)
                    dve.wait_ge(hg_copied, t + 1)
                    nc.vector.tensor_tensor(hs[:, LO, bass.ds(t, 1), 0:D], ps[:, h, 0:D],
                                            hs[:, HI, bass.ds(t, 1), 0:D], ALU.subtract)
                    nc.vector.tensor_tensor(vab[:, bass.ds(t, 1), :], ps[:, g, V:V + 2], bab[:, :], ALU.add)
                    nc.vector.tensor_tensor(gs[:, LO, bass.ds(t, 1), 0:U + 2], ps[:, g, 0:U + 2],
                                            gs[:, HI, bass.ds(t, 1), 0:U + 2], ALU.subtract).then_inc(hg_split, 1)
            dve.wait_ge(cols_copied, T)
            nc.vector.tensor_reduce(top[:, 0:1], srs[:, 1, :], mybir.AxisListType.X, ALU.max).then_inc(top_local, 1)
            dve.wait_ge(top_spread, 1)
            nc.vector.tensor_reduce(top[:, 1:2], ps[:, TOP_BANK, 0:P], mybir.AxisListType.X, ALU.max
                                    ).then_inc(top_local, 1)
            dve.wait_ge(top_local, 2)
            nc.vector.tensor_scalar(srs[:, 1, :], srs[:, 1, :], top[:, 1:2], E_EXP * math.log(2.0), ALU.subtract,
                                    ALU.add)
            nc.vector.tensor_scalar(row_eps[:, :], row_eps[:, :], SLOPE, top[:, 1:2], ALU.mult, ALU.subtract
                                    ).then_inc(shifted, 1)
            dve.wait_ge(tables_ready, 1)
            dve.wait_ge(biases_loaded, 16 * (1 + LAYERS))
            dve.wait_ge(x_kept, T)
            dve.wait_ge(sl_copied, C + 1)

            def split_weights_lo(l):
                dve.wait_ge(w_hi, l + 1)
                nc.vector.scalar_tensor_tensor(out=wL[:, l, LO, :, :], in0=wt(l) if l else w1_raw,
                                               scalar=2.0 ** W_EXP, in1=wL[:, l, HI, :, :], op0=ALU.mult,
                                               op1=ALU.subtract).then_inc(w_split, 1)

            def relu(c, jt):
                dve.wait_ge(rest_ready, c * T + jt + 1)
                nc.vector.tensor_scalar(lr[:, jt % TC, :], sl[:, bass.ds(c * CI, CI)], srs[:, 0, jt:jt + 1], 0.0,
                                        ALU.add, ALU.max).then_inc(dve_relu_ready, 1)

            def rest(c, jt):
                dve.wait_ge(exp_done, c * T + jt + 1)
                nc.vector.tensor_tensor(er[:, jt % RING, LO, :], lr[:, jt % TC, :], er[:, jt % RING, HI, :],
                                        ALU.subtract).then_inc(rest_ready, 1)

            def mask(c, jt):
                dve.wait_ge(rest_ready, c * T + jt + TC + 1)
                nc.vector.tensor_tensor(er[:, jt % RING, :, :], er[:, jt % RING, :, :],
                                        adjT[:, bass.ds(c, 1), jt, :].broadcast_to([P, 2, CI]),
                                        ALU.mult).then_inc(e_ready, 1)

            def take_aggregate(c, behind):
                if behind:
                    dve.wait_ge(xn_ready, c * TC)
                dve.wait_ge(xb_done, c + 1)
                nc.vector.tensor_tensor(ab[:, :, :], ps[:, 0:TC, U:U + 2], vab[:, bass.ds(c * TC, TC), :],
                                        ALU.add).then_inc(ab_ready, 1)
                nc.vector.tensor_copy(bscale[:, 1, bass.ds(c * TC, TC)], ps[:, 0:TC, ONE])
                nc.vector.tensor_scalar(scale[:, 2, bass.ds(c * TC, TC)], ps[:, 0:TC, ONE], DEG_EPS, None,
                                        ALU.add)
                for it in range(TC):
                    ins = nc.vector.tensor_tensor(y[:, it, :], ps[:, it, 0:D], bias[:, 0, :], ALU.add)
                ins.then_inc(xb_read, 1)

            def gate(c, chain):
                dve.wait_ge(ab_tanh, c + 1)
                chain(nc.vector.tensor_scalar(ab[:, :, :], ab[:, :, :], 0.5, 0.5, ALU.mult, ALU.add))
                chain.wait()
                dve.wait_ge(xb_read, c + 2)
                for it in range(TC):
                    ins = nc.vector.tensor_scalar(y[:, it, :], y[:, it, :], ab[:, it, 1:2], None, ALU.mult)
                chain(ins)

            def add_attention(c, chain):
                dve.wait_ge(eps_ready, 1)
                dve.wait_ge(e_used, (c + 1) * T + RING)
                chain(nc.vector.scalar_tensor_tensor(out=rd[:, :], in0=row_eps[:, bass.ds(c * TC, TC)],
                                                     scalar=DEN_EPS * 2.0 ** E_EXP, in1=ps[:, XA:XA + TC, D],
                                                     op0=ALU.mult, op1=ALU.add))
                chain.wait()
                chain(nc.vector.reciprocal(rd[:, :], rd[:, :]))
                chain.wait()
                chain(nc.vector.tensor_tensor(rd[:, :], rd[:, :], ab[:, :, 0], ALU.mult))
                chain.wait()
                for it in range(TC):
                    nc.vector.scalar_tensor_tensor(out=y[:, it, :], in0=ps[:, XA + it, 0:D],
                                                   scalar=rd[:, it:it + 1], in1=y[:, it, :],
                                                   op0=ALU.mult, op1=ALU.add).then_inc(sum_ready, 1)

            def variance_0(c, chain):
                for it in range(TC):
                    dve.wait_ge(sum_tanh, c * TC + it + 1)
                    ins = nc.vector.scalar_tensor_tensor(out=y[:, it, :], in0=y[:, it, :], scalar=0.5,
                                                         in1=x32[:, bass.ds(c * TC + it, 1), :],
                                                         op0=ALU.mult, op1=ALU.add)
                chain(ins)
                chain.wait()
                for it in range(TC):
                    ins = nc.vector.bn_stats(st[:, it, :], y[:, it, :])
                chain(ins)
                chain.wait()
                dve.nop(nofuse=True)
                for it in range(TC):
                    ins = nc.vector.bn_aggr(mv[:, it, :], st[:, it, :])
                chain(ins)
                chain.wait()
                nc.vector.tensor_scalar(rs[:, :], mv[:, :, 1], LN_EPS, None, ALU.add).then_inc(var_ready, 1)

            def normalise_0(c):
                dve.wait_ge(rs_ready, c + 1)
                for it in range(TC):
                    nc.vector.tensor_scalar(x32[:, bass.ds(c * TC + it, 1), :], y[:, it, :], mv[:, it, 0:1],
                                            rs[:, it:it + 1], ALU.subtract, ALU.mult).then_inc(xn_ready, 1)

            def split_lo_0(c):
                for it in range(TC):
                    t = c * TC + it
                    dve.wait_ge(hi_ready, t + 1)
                    nc.vector.tensor_tensor(xs[:, 0, LO, bass.ds(t, 1), :], x32[:, bass.ds(t, 1), :],
                                            xs[:, 0, HI, bass.ds(t, 1), :], ALU.subtract).then_inc(split_ready, 1)

            def chunk_0(c, chain, tail):
                for jt in range(T):
                    if (jt + DVE_SLOT) % TC == DVE_SLOT:
                        relu(c, jt + DVE_SLOT)
                    rest(c, jt)
                    if jt < LAYERS and not tail:
                        split_weights_lo(jt)
                    if jt > 0:
                        mask(c, jt - 1)
                    if jt == SUM_AT and tail:
                        add_attention(c - 1, chain)
                    if jt == NORM_AT and tail:
                        variance_0(c - 1, chain)
                    if jt == NORM_AT + 1 and tail:
                        normalise_0(c - 1)
                    if jt == AGG_AT:
                        take_aggregate(c, tail)
                    if jt == LO_AT and tail:
                        split_lo_0(c - 1)
                    if jt == GATED_AT:
                        gate(c, chain)
                mask(c, T - 1)

            chain = Chain()
            chunk_0(0, chain, False)
            chain.end()
            with dve.Fori(1, C) as c:
                chain = Chain(c - 1, 8)
                chunk_0(c, chain, True)
            chain.end(C - 1)
            chain = Chain()
            dve.wait_ge(dis_ready, 1)
            chain(nc.vector.tensor_scalar(zscale[:, 2, :], scale[:, 2, :], 2.0 ** -W_EXP, None, ALU.mult))
            add_attention(C - 1, chain)
            variance_0(C - 1, chain)
            normalise_0(C - 1)
            split_lo_0(C - 1)
            chain.end()
            def split_yt(s):
                for k in range(K):
                    dve.wait_ge(yt_hi, K * s + k + 1)
                    nc.vector.tensor_tensor(YT[:, LO, k, :], ps[:, bass.ds((s % 2) * K + k, 1), :],
                                            YT[:, HI, k, :], ALU.subtract).then_inc(yt_split, 1)

            def norm(s, chain, last):
                l, c = split_step(s, LAYERS if last else LAYERS - 1)
                pairs = [(0, 1), (2, 3)]
                dve.wait_ge(xn_ready, T + s * TC)
                for n, pair in enumerate(pairs):
                    for it in pair:
                        dve.wait_ge(z_done, s * TC + it + 1)
                        dve.wait_ge(bias_added, s * TC + it + 2)
                        chain(nc.vector.scalar_tensor_tensor(
                            out=v[:, it, :], in0=ps[:, Z_BANK + it, 0:D],
                            scalar=zscale[:, bass.ds(l, 1), bass.ds(c * TC + it, 1)],
                            in1=x32[:, bass.ds(c * TC + it, 1), :], op0=ALU.mult, op1=ALU.add))
                    for it in pair:
                        chain.wait(1 - it % 2)
                        ins = nc.vector.bn_stats(st[:, it, :], v[:, it, :])
                    chain(ins)
                    chain.wait()
                    dve.nop(nofuse=True)
                    for it in pair:
                        ins = nc.vector.bn_aggr(mv[:, it, :], st[:, it, :])
                    chain(ins)
                    chain.wait()
                    nc.vector.tensor_scalar(rs[:, 2 * n:2 * n + 2], mv[:, 2 * n:2 * n + 2, 1], LN_EPS, None,
                                            ALU.add).then_inc(var_ready, 1)
                for n, pair in enumerate(pairs):
                    dve.wait_ge(rs_ready, C + 2 * s + n + 1)
                    for it in pair:
                        nc.vector.tensor_scalar(x32[:, bass.ds(c * TC + it, 1), :], v[:, it, :], mv[:, it, 0:1],
                                                rs[:, it:it + 1], ALU.subtract, ALU.mult).then_inc(xn_ready, 1)
                for it in range(0 if last else TC):
                    t = c * TC + it
                    dve.wait_ge(hi_ready, T + s * TC + it + 1)
                    nc.vector.scalar_tensor_tensor(
                        out=xs[:, bass.ds((l + 1) % 2, 1), LO, bass.ds(t, 1), :],
                        in0=x32[:, bass.ds(t, 1), :], scalar=scale[:, bass.ds(l + 1, 1), bass.ds(t, 1)],
                        in1=xs[:, bass.ds((l + 1) % 2, 1), HI, bass.ds(t, 1), :],
                        op0=ALU.mult, op1=ALU.subtract).then_inc(split_ready, 1)

            with dve.Fori(0, STEPS - C) as s:
                chain = Chain(s, 8)
                split_yt(s)
                norm(s, chain, False)
            chain.end(STEPS - C)
            with dve.Fori(STEPS - C, STEPS) as s:
                chain = Chain(s - (STEPS - C), 8)
                split_yt(s)
                norm(s, chain, True)
            chain.end(C)

        @block.tensor
        def _(pe):
            pe.sem_inc(e_used, RING)
            pe.wait_ge(ident_ready, 3)

            def transpose_x(c, it):
                pe.wait_ge(x_loaded[it], 16 * (c + 1))
                pe.wait_ge(xT_copied, c * TC + it + 1)
                for k in range(K):
                    ins = pe.transpose(ps[:, X_BANK, k * P:(k + 1) * P], x_in[:, it, k * P:(k + 1) * P],
                                       ident[:, :])
                ins.then_inc(x_transposed, 1)

            def load_tile(c, it, ahead):
                t = c * TC + it
                pe.wait_ge(xT_copied, t + 2)
                pe.wait_ge(hg_split, t + 1)
                for bank, w, width in ((h_bank(it), wH, HW), (g_bank(it), wG, GW)):
                    for k in range(K):
                        ins = pe.matmul(ps[:, bank, 0:width], xT[:, k, it, :], w[:, k, :], start=(k == 0),
                                        stop=(k == K - 1))
                    ins.then_inc(hg_done, 1)
                if ahead:
                    transpose_x(c + (it + 1) // TC, (it + 1) % TC)
                for part in range(2):
                    pe.wait_ge(adj_cast, 2 * t + part + 1)
                    pe.wait_ge(act_copied if part else dve_copied, t + 1)
                    for jt in range(part * HALF, (part + 1) * HALF):
                        ins = pe.transpose(blocks(part)[:, jt % HALF, :], adj16[:, it % 2, jt * P:(jt + 1) * P],
                                           ident16[:, :])
                    ins.then_inc(adj_transposed, 1)
                if it == TC - 1:
                    pe.wait_ge(cols_copied, t + 1)
                    pe.wait_ge(sl_copied, c + 1)
                    for i in range(TC):
                        ins = pe.matmul(ps[:, S_BANK, i * P:(i + 1) * P], sl_col[:, i:i + 1].broadcast_to([P, P]),
                                        ident[:, :], start=True, stop=True)
                    ins.then_inc(sl_done, 1)

            transpose_x(0, 0)
            pe.wait_ge(folded, 2 * K)
            pe.wait_ge(gcn_weights, 16 * 5)
            with pe.Fori(0, C - 1) as c:
                for it in range(TC):
                    load_tile(c, it, True)
            for it in range(TC):
                load_tile(C - 1, it, it + 1 < TC)

            def transpose_weights(l):
                for ki in range(K):
                    for ko in range(K):
                        ins = pe.transpose(wt(l)[:, ki, ko * P:(ko + 1) * P],
                                           w_raw[:, l - 1, ko, ki * P:(ki + 1) * P], ident[:, :])
                ins.then_inc(w_transposed, 1)

            def aggregate_G(c, tiles):
                for jt in tiles:
                    for it in range(TC):
                        for part in (HI, LO):
                            ins = pe.matmul(ps[:, it, 0:GW], adjT[:, bass.ds(c, 1), jt, it * P:(it + 1) * P],
                                            gs[:, part, jt, :], start=(jt == 0 and part == HI),
                                            stop=(jt == T - 1 and part == LO))
                return ins

            def attend(c):
                for jt in range(T):
                    pe.wait_ge(e_ready, c * T + jt + 1)
                    for it in range(TC):
                        for n, (e_part, h_part) in enumerate(PARTS):
                            width = D + 1 if h_part == HI else D
                            ins = pe.matmul(ps[:, XA + it, 0:width], er[:, jt % RING, e_part, it * P:(it + 1) * P],
                                            hs[:, h_part, jt, 0:width], start=(jt == 0 and n == 0),
                                            stop=(jt == T - 1 and n == len(PARTS) - 1))
                    ins.then_inc(e_used, 1)

            pe.wait_ge(square_weights, 16 * (LAYERS - 1))
            pe.wait_ge(xT_copied, T + 1)
            transpose_weights(1)
            pe.wait_ge(act_copied, T + 1)
            pe.wait_ge(dve_copied, T + 1)
            pe.wait_ge(hg_split, T + 1)
            pe.wait_ge(tables_ready, 1)
            aggregate_G(0, range(0, 2))
            pe.wait_ge(hg_split, T + 2)
            pe.wait_ge(top_local, 1)
            pe.matmul(ps[:, TOP_BANK, 0:P], top[:, 0:1].broadcast_to([P, P]), ident[:, :], start=True,
                      stop=True).then_inc(top_spread, 1)
            transpose_weights(2)
            aggregate_G(0, range(2, T)).then_inc(xb_done, 1)
            pe.wait_ge(sl_copied, C + 1)
            pe.wait_ge(shifted, 1)
            pe.wait_ge(w_split, LAYERS)
            attend(0)
            with pe.Fori(1, C) as c:
                pe.wait_ge(xb_read, c + 1)
                aggregate_G(c, range(T)).then_inc(xb_done, 1)
                pe.wait_ge(sum_ready, c * TC + 1)
                attend(c)

            def aggregate(s, k, tiles):
                l, c = split_step(s)
                for jt in tiles:
                    for part in (HI, LO):
                        ins = pe.matmul(ps[:, bass.ds((s % 2) * K + k, 1), :],
                                        xs[:, bass.ds(l % 2, 1), part, jt, k * P:(k + 1) * P],
                                        adjT[:, bass.ds(c, 1), jt, :],
                                        start=(jt == 0 and part == HI), stop=(jt == T - 1 and part == LO))
                return ins

            def project(s):
                pe.wait_ge(yt_split, K * (s + 1))
                pe.wait_ge(var_ready, C + 2 * s)
                for it in range(TC):
                    for k in range(K):
                        for n, (y_part, w_part) in enumerate(PARTS):
                            ins = pe.matmul(ps[:, Z_BANK + it, 0:D], YT[:, y_part, k, it * P:(it + 1) * P],
                                            wL[:, bass.ds(split_step(s)[0], 1), w_part, k, :],
                                            start=(k == 0 and n == 0), stop=(k == K - 1 and n == len(PARTS) - 1))
                    ins.then_inc(z_done, 1)

            START, FIRST, REST = range(TC + 2), range(T - TC), range(T - TC, T)

            def step(s, project_last):
                pe.wait_ge(split_ready, split_step(s)[0] * T + (T - TC))
                aggregate(s, 0, START)
                if project_last:
                    project(s - 1)
                aggregate(s, 0, FIRST[len(START):])
                aggregate(s, 1, FIRST)
                pe.wait_ge(split_ready, split_step(s)[0] * T + T)
                for k in range(K):
                    aggregate(s, k, REST).then_inc(yt_done, 1)

            step(0, False)
            with pe.Fori(1, STEPS) as s:
                step(s, True)
            pe.wait_ge(var_ready, C + 2 * (STEPS - 1))
            for k in range(K):
                pe.wait_ge(yt_split, K * (STEPS - 1) + k + 1)
                for it in range(TC):
                    for n, (y_part, w_part) in enumerate(PARTS):
                        ins = pe.matmul(ps[:, Z_BANK + it, 0:D], YT[:, y_part, k, it * P:(it + 1) * P],
                                        wL[:, LAYERS - 1, w_part, k, :], start=(k == 0 and n == 0),
                                        stop=(k == K - 1 and n == len(PARTS) - 1))
                    if k == K - 1:
                        ins.then_inc(z_done, 1)


_INS = ['x', 'adj', 'L0_gnn_W_sa', 'L0_gnn_a_sa', 'L0_gnn_W_gcnb', 'L0_gnn_b_gcnb', 'L0_gnn_Wa', 'L0_gnn_ba',
        'L0_gnn_Wb', 'L0_gnn_bb', 'L1_gnn_W', 'L1_gnn_b', 'L2_gnn_W', 'L2_gnn_b', 'L3_gnn_W', 'L3_gnn_b']


def kernel(**inputs):
    import numpy as _np
    import concourse.bacc as _bacc
    from concourse import mybir as _mybir
    from concourse.bass_utils import run_bass_kernel_spmd as _run

    nc = _bacc.Bacc("TRN2", target_bir_lowering=False, num_devices=1)
    arrays, args = {}, []
    for name in _INS:
        a = _np.ascontiguousarray(inputs[name])
        arrays[f"in_{name}_dram"] = a
        args.append(nc.dram_tensor(f"in_{name}_dram", a.shape, _mybir.dt.from_np(a.dtype), kind="ExternalInput").ap())
    shape = inputs['x'].shape
    args.append(nc.dram_tensor("out_0_dram", shape, _mybir.dt.float32, kind="ExternalOutput").ap())
    build(nc, *args)
    r = _run(nc, [arrays], core_ids=[0])
    return r.results[0]["out_0_dram"]
```

```python
import math
from contextlib import ExitStack

import concourse.bass as bass
from concourse import mybir

F32 = mybir.dt.float32
F16 = mybir.dt.float16
ALU = mybir.AluOpType
ACT = mybir.ActivationFunctionType

P = 128
CI = 512
LN_EPS = 1e-5
DEN_EPS = 1e-5
DEG_EPS = 1e-8
SLOPE = 0.01
E_EXP = 15
W_EXP = 6
HI, LO = 0, 1
PARTS = ((HI, HI), (HI, LO), (LO, HI))


def build(nc, x, adj, W_sa, a_sa, W_gcnb, b_gcnb, Wa, ba, Wb, bb, W1, b1, W2, b2, W3, b3, out):
    N, D = x.shape
    T = N // P
    K = D // P
    C = N // CI
    TC = CI // P
    HALF = T // 2
    RING = T
    XS = 2 * TC
    HEADS = W1.shape[0]
    LAYERS = 3
    STEPS = LAYERS * C
    HW = D + 2
    U, ONE, V = D, D + 2, D + 2
    GW = D + 4

    with ExitStack() as ctx:
        def sb(name, shape, dt=F32):
            return ctx.enter_context(nc.sbuf_tensor(name, shape, dt))

        def sem(name):
            return ctx.enter_context(nc.semaphore(name))

        adjT = sb("adjT", [P, C, T, CI], F16)
        region = sb("region", [P, 2 * T * D + RING * 2 * CI], F16)
        xs = region[:, 0:4 * T * D].rearrange("p (l h t d) -> p l h t d", l=2, h=2, t=T)
        adj16 = region[:, 0:TC * N].rearrange("p (s n) -> p s n", s=TC)
        er = region[:, 2 * T * D:2 * T * D + RING * 2 * CI].rearrange("p (s h n) -> p s h n", s=RING, h=2)
        x_in = sb("x_in", [P, XS, D])
        v = x_in[:, TC:XS, :]
        w_raw = v.rearrange("p (l k) n -> p l k n", k=K)
        xT = sb("xT", [P, 2, 2, K, P], F16)
        x32 = sb("x32", [P, T, D])
        hs = sb("hs", [P, 2, T, HW], F16)
        gs = sb("gs", [P, 2, T, GW], F16)
        sl = sb("sl", [P, N])
        YT = sl[:, 0:K * CI].bitcast(F16).rearrange("p (h k n) -> p h k n", h=2, k=K)
        products = sl[:, 0:2 * K * D].rearrange("p (k d) -> p k d", d=D)
        lr = sb("lr", [P, TC, CI])
        a_bc = lr[:, 2, :]
        w1_raw = lr[:, 3, :].rearrange("p (k n) -> p k n", k=K)
        w_early = er[:, T // 2:T, :, :].rearrange("p s h n -> p (s h n)").bitcast(F32)
        wH = w_early[:, 0:K * HW].rearrange("p (k n) -> p k n", k=K)
        wG = w_early[:, K * HW:K * (HW + GW)].rearrange("p (k n) -> p k n", k=K)
        wH16 = sb("wH16", [P, 2, K, HW], F16)
        wG16 = sb("wG16", [P, 2, K, GW], F16)
        wL = sb("wL", [P, LAYERS, 2, K, D], F16)
        bias = sb("bias", [P, 1 + LAYERS, D])
        bab = sb("bab", [P, 2])
        ident = sb("ident", [P, P])
        ident16 = sb("ident16", [P, P], F16)
        sl_col = sb("sl_col", [P, TC])
        srs = sb("srs", [P, 2, T])
        row_eps = sb("row_eps", [P, T])
        top = sb("top", [P, 2])
        vab = sb("vab", [P, T, 2])
        scale = sb("scale", [P, LAYERS, T])
        zscale = sb("zscale", [P, LAYERS, T])
        bscale = sb("bscale", [P, LAYERS, T])
        btmp = sb("btmp", [P, D])
        half = sb("half", [P, D])
        minus_half = sb("minus_half", [P, T])
        ab = sb("ab", [P, 2 * TC, 2])
        rd = sb("rd", [P, TC])
        st = sb("st", [P, TC, 6])
        mv = sb("mv", [P, TC, 2])
        rs = sb("rs", [P, TC])

        ps = ctx.enter_context(nc.psum_tensor("ps", [P, 8, CI], F32))
        X_BANK, S_BANK = 6, 7
        TOP_BANK = X_BANK
        XA = TC
        Z_BANK = 4

        def blocks(part):
            return ps[:, TC + part, :].bitcast(F16).rearrange("p (r n) -> p r n", n=P)

        def h_bank(t):
            return 2 * (t % 2)

        def g_bank(t):
            return h_bank(t) + 1

        def wt(l):
            return ps[:, X_BANK if l == 1 else S_BANK, :].rearrange("p (k n) -> p k n", k=K)

        def y(c, it):
            return x_in[:, bass.ds((c % 2) * TC + it, 1), :]

        def gates(c):
            return ab[:, bass.ds((c % 2) * TC, TC), :]

        x_loaded = [sem(f"x_loaded{i}") for i in range(XS)]
        adj_loaded = [sem(f"adj_loaded{i}") for i in range(TC)]
        sa_weights = sem("sa_weights")
        gcn_weights = sem("gcn_weights")
        bab_loaded = sem("bab_loaded")
        square_weights = sem("square_weights")
        w1_loaded = sem("w1_loaded")
        biases_loaded = sem("biases_loaded")
        ident_ready = sem("ident_ready")
        tables_ready = sem("tables_ready")
        folded = sem("folded")
        cols_copied = sem("cols_copied")
        top_local = sem("top_local")
        top_spread = sem("top_spread")
        shifted = sem("shifted")
        w_transposed = sem("w_transposed")
        w_hi = sem("w_hi")
        w_split = sem("w_split")
        x_transposed = sem("x_transposed")
        xT_hi = sem("xT_hi")
        xT_split = sem("xT_split")
        early_hi = sem("early_hi")
        early_split = sem("early_split")
        x_kept = sem("x_kept")
        adj_transposed = sem("adj_transposed")
        blocks_copied = [sem(f"blocks_copied{i}") for i in range(2)]
        hg_done = sem("hg_done")
        hg_copied = sem("hg_copied")
        hg_split = sem("hg_split")
        sl_done = sem("sl_done")
        sl_copied = sem("sl_copied")
        eps_ready = sem("eps_ready")
        xb_done = sem("xb_done")
        xb_read = sem("xb_read")
        relu_ready = sem("relu_ready")
        dve_relu_ready = sem("dve_relu_ready")
        exp_done = sem("exp_done")
        rest_ready = sem("rest_ready")
        e_ready = sem("e_ready")
        e_used = sem("e_used")
        ab_ready = sem("ab_ready")
        ab_tanh = sem("ab_tanh")
        gates_ready = sem("gates_ready")
        y_gated = sem("y_gated")
        sum_ready = sem("sum_ready")
        sum_tanh = sem("sum_tanh")
        xn_ready = sem("xn_ready")
        hi_ready = sem("hi_ready")
        split_ready = sem("split_ready")
        var_ready = sem("var_ready")
        rs_ready = sem("rs_ready")
        dis_ready = sem("dis_ready")
        bias_temp = sem("bias_temp")
        bias_added = sem("bias_added")
        yt_done = sem("yt_done")
        yt_hi = sem("yt_hi")
        yt_split = sem("yt_split")
        z_done = sem("z_done")
        dve_done = sem("dve_done")
        stored = sem("stored")

        x_t = x.rearrange("(t p) d -> t p d", p=P)
        adj_t = adj.rearrange("(t p) n -> t p n", p=P)
        out_t = out.rearrange("(t p) d -> t p d", p=P)
        out_p = out.rearrange("(c t p) d -> c p t d", p=P, t=2)

        def split_step(s, layers=LAYERS):
            layer = s // C
            if not isinstance(layer, int):
                layer = layer.with_bounds(min_val=0, max_val=layers - 1)
            return layer, s % C

        def row(v1):
            return v1.rearrange("(a n) -> a n", a=1)

        DVE_SLOT = 2
        ACT_RELUS = T - T // TC

        def act_relus(jt):
            return jt + 1 - (jt + TC - DVE_SLOT) // TC

        GATE_AT, GATED_AT = 2, 3
        SUM_AT, TANH_AT, VAR_AT, NORM_AT, HI_AT, AGG_AT = 8, 10, 11, 12, 14, 15
        LOADED_AT, GATE_0_AT, GATED_0_AT = T // 2 - 2, T // 2, T // 2 + 1
        W1_AT, W_AT = 0, T // 2 + 2

        block = ctx.enter_context(nc.Block())

        @block.sync
        def _(sp):
            def load_x(t):
                if t >= XS:
                    sp.wait_ge(x_transposed, t - XS + 1)
                    sp.wait_ge(x_kept, t - XS + 1)
                sp.dma_start(x_in[:, t % XS, :], x_t[t]).then_inc(x_loaded[t % XS], 16)

            load_x(0)
            sp.dma_start(a_bc, a_sa.broadcast_to([P, 2 * D])).then_inc(sa_weights, 16)
            sp.dma_start(wG[:, :, 0:D], W_gcnb.rearrange("(k p) e -> p k e", p=P)).then_inc(gcn_weights, 16)
            for t in range(1, T):
                load_x(t)
            sp.wait_ge(x_transposed, T)
            sp.wait_ge(x_kept, T)
            for l, w in ((1, W2), (2, W3)):
                sp.dma_start(w_raw[:, l - 1], w.rearrange("(k p) i -> p k i", p=P)).then_inc(square_weights, 16)
            for t in range(0, T - 2, 2):
                sp.wait_ge(xn_ready, LAYERS * T + t + 2)
                sp.dma_start(out_p[t // 2], x32[:, t:t + 2, :]).then_inc(stored, 16)
            for t in range(T - 2, T):
                sp.wait_ge(xn_ready, LAYERS * T + t + 1)
                sp.dma_start(out_t[t], x32[:, t, :]).then_inc(stored, 16)
            sp.wait_ge(stored, 16 * (T // 2 + 1))

        @block.gpsimd
        def _(pool):
            def load_adj(c, it, behind=True):
                t = c * TC + it
                if behind:
                    pool.wait_ge(adj_transposed, 2 * (t - TC + 1))
                pool.dma_start(adj16[:, it, :], adj_t[t]).then_inc(adj_loaded[it], 16)

            nc.gpsimd.memset(ident[:, :], 0.0).then_inc(ident_ready, 1)
            pool.wait_ge(ident_ready, 1)
            nc.gpsimd.affine_select(out=ident[:, :], in_=ident[:, :], compare_op=ALU.not_equal, fill=1.0,
                                    base=0, pattern=[[-1, P]], channel_multiplier=1).then_inc(ident_ready, 1)
            pool.wait_ge(ident_ready, 2)
            nc.gpsimd.tensor_copy(ident16[:, :], ident[:, :]).then_inc(ident_ready, 1)
            nc.gpsimd.memset(half[:, :], 0.5)
            nc.gpsimd.memset(minus_half[:, :], -0.5)
            nc.gpsimd.memset(hs[:, HI, :, D:D + 1], 1.0)
            nc.gpsimd.memset(gs[:, HI, :, ONE:ONE + 1], 1.0)
            nc.gpsimd.memset(scale[:, 0:2, :], 1.0)
            nc.gpsimd.memset(zscale[:, 0:2, :], 2.0 ** -W_EXP)
            nc.gpsimd.memset(bscale[:, 0:1, :], 1.0)
            nc.gpsimd.memset(bscale[:, 2:3, :], 1.0).then_inc(tables_ready, 1)
            pool.wait_ge(tables_ready, 1)
            pool.wait_ge(gcn_weights, 16 * 5)
            for n, b in enumerate((ba, bb)):
                pool.dma_start(bab[:, n:n + 1], row(b).broadcast_to([P, 1])).then_inc(bab_loaded, 16)
            for it in range(TC):
                load_adj(0, it, False)

            with pool.Fori(0, T // XS) as r:
                for i in range(XS):
                    pool.wait_ge(x_loaded[i], 16 * (r + 1))
                    nc.gpsimd.tensor_tensor(x32[:, bass.ds(r * XS + i, 1), :], x_in[:, i:i + 1, :],
                                            half[:, :].rearrange("p (o d) -> p o d", o=1), ALU.add
                                            ).then_inc(x_kept, 1)
                    if i % 2 == 1:
                        load_adj(r + 1, i // 2)
            for k in range(K):
                pool.dma_start(w1_raw[:, k, :].rearrange("p (h e) -> p h e", h=HEADS),
                               W1[:, k * P:(k + 1) * P, :].rearrange("h p e -> p h e")).then_inc(w1_loaded, 16)
            for n, b in enumerate((b_gcnb, b1.rearrange("h e -> (h e)"), b2, b3)):
                pool.dma_start(bias[:, n, :], row(b).broadcast_to([P, D])).then_inc(biases_loaded, 16)
            for it in range(TC):
                load_adj(C - 1, it)
            pool.wait_ge(biases_loaded, 16 * (1 + LAYERS))
            pool.sem_inc(bias_added, 1)

            def inverse_root(count, a, b):
                pool.wait_ge(var_ready, count)
                nc.gpsimd.tensor_tensor(rs[:, a:b], rs[:, a:b], minus_half[:, a:b], ALU.pow).then_inc(rs_ready, 1)

            def add_bias(n, l, t):
                pool.wait_ge(split_ready, n + 1)
                pool.wait_ge(bias_added, n + 1)
                nc.gpsimd.tensor_tensor(btmp[:, :], bias[:, bass.ds(l + 1, 1), :],
                                        bscale[:, bass.ds(l, 1), bass.ds(t, 1)].broadcast_to([P, 1, D]),
                                        ALU.mult).then_inc(bias_temp, 1)
                pool.wait_ge(bias_temp, n + 1)
                pool.nop(nofuse=True)
                nc.gpsimd.tensor_tensor(x32[:, bass.ds(t, 1), :], x32[:, bass.ds(t, 1), :], btmp[:, :],
                                        ALU.add).then_inc(bias_added, 1)

            def gate_sum(c):
                pool.wait_ge(gates_ready, c + 1)
                pool.wait_ge(xb_read, (c + 1) * TC)
                pool.nop(nofuse=True)
                for it in range(TC):
                    nc.gpsimd.tensor_tensor(y(c, it), y(c, it),
                                            ab[:, bass.ds((c % 2) * TC + it, 1), 1:2].broadcast_to([P, 1, D]),
                                            ALU.mult).then_inc(y_gated, 1)

            gate_sum(0)
            with pool.Fori(1, C) as c:
                gate_sum(c)
                inverse_root(c, 0, TC)
                for it in range(TC):
                    t = (c - 1) * TC + it
                    pool.wait_ge(hi_ready, t + 1)
                    pool.nop(nofuse=True)
                    nc.gpsimd.tensor_tensor(xs[:, 0, LO, bass.ds(t, 1), :], x32[:, bass.ds(t, 1), :],
                                            xs[:, 0, HI, bass.ds(t, 1), :], ALU.subtract).then_inc(split_ready, 1)
                for it in range(TC):
                    add_bias((c - 1) * TC + it, 0, (c - 1) * TC + it)
            pool.wait_ge(xb_read, T)
            nc.gpsimd.tensor_tensor(scale[:, 2, :], scale[:, 2, :], minus_half[:, :], ALU.pow
                                    ).then_inc(dis_ready, 1)
            inverse_root(C, 0, TC)
            for it in range(TC):
                add_bias((C - 1) * TC + it, 0, (C - 1) * TC + it)
            with pool.Fori(0, STEPS - C) as s:
                l, c = split_step(s, LAYERS - 1)
                for pair in range(TC // 2):
                    inverse_root(C + 2 * s + pair + 1, 2 * pair, 2 * pair + 2)
                for it in range(TC):
                    add_bias(T + s * TC + it, l + 1, c * TC + it)
            with pool.Fori(STEPS - C, STEPS) as s:
                for pair in range(TC // 2):
                    inverse_root(C + 2 * s + pair + 1, 2 * pair, 2 * pair + 2)

        @block.scalar
        def _(act):
            act.dma_start(wH[:, :, 0:D], W_sa.rearrange("(k p) e -> p k e", p=P)).then_inc(sa_weights, 16)
            for n, w in enumerate((Wa, Wb)):
                for part in range(2):
                    act.dma_start(wG[:, :, D + 2 * part + n],
                                  w[0, part * D:(part + 1) * D].rearrange("(k p) -> p k", p=P),
                                  allow_slow_non_contiguous=True).then_inc(gcn_weights, 16)
            act.sem_inc(blocks_copied[1], 1)
            act.sem_inc(sl_copied, 1)

            def copy_x(t, i):
                act.wait_ge(x_transposed, t + 1)
                nc.scalar.activation(xT[:, i % 2, HI, :, :], ps[:, X_BANK, 0:D].rearrange("p (k n) -> p k n", k=K),
                                     ACT.Copy).then_inc(xT_hi, 1)

            def take_hi(t, i):
                act.wait_ge(hg_done, 2 * t + 1)
                act.nop(nofuse=True)
                nc.scalar.activation(hs[:, HI, bass.ds(t, 1), 0:D], ps[:, h_bank(i), 0:D], ACT.Copy,
                                     scale=2.0 ** -W_EXP)
                act.wait_ge(hg_done, 2 * t + 2)
                act.nop(nofuse=True)
                nc.scalar.activation(gs[:, HI, bass.ds(t, 1), 0:U + 2], ps[:, g_bank(i), 0:U + 2],
                                     ACT.Copy, scale=2.0 ** -W_EXP).then_inc(hg_copied, 1)

            def spread_s_left(q):
                act.wait_ge(sl_done, q + 2)
                act.nop(nofuse=True)
                nc.scalar.activation(sl[:, bass.ds(q * CI, CI)], ps[:, S_BANK, :], ACT.Copy,
                                     scale=1.0 - SLOPE).then_inc(sl_copied, 1)

            def take_blocks(c, it):
                t = c * TC + it
                act.wait_ge(adj_transposed, 2 * t + 2)
                act.nop(nofuse=True)
                nc.scalar.activation(adjT[:, bass.ds(c, 1), HALF:T, it * P:(it + 1) * P], blocks(1),
                                     ACT.Copy).then_inc(blocks_copied[1], 1)

            def take_last(c, it):
                take_blocks(c, it)
                if it % 2 == 1:
                    spread_s_left(2 * c + it // 2)

            def load_chunk(c, last):
                for it in range(TC):
                    for i in (2 * it, 2 * it + 1):
                        if i + 1 < XS or not last:
                            copy_x(c * XS + i + 1, i + 1)
                        if i % 2 == 0 and it > 0:
                            take_last(c, it - 1)
                        take_hi(c * XS + i, i)
                take_last(c, TC - 1)

            act.wait_ge(folded, 2 * K)
            nc.scalar.activation(wH16[:, HI, :, :], wH, ACT.Copy, scale=2.0 ** W_EXP).then_inc(early_hi, 1)
            copy_x(0, 0)
            act.wait_ge(gcn_weights, 16 * 5)
            nc.scalar.activation(wG16[:, HI, :, :], wG, ACT.Copy, scale=2.0 ** W_EXP).then_inc(early_hi, 1)
            with act.Fori(0, C // 2 - 1) as c:
                load_chunk(c, False)
            load_chunk(C // 2 - 1, True)

            def split_weights_hi(l):
                if l == 0:
                    act.wait_ge(w1_loaded, 16 * K)
                else:
                    act.wait_ge(w_transposed, l)
                nc.scalar.activation(wL[:, l, HI, :, :], wt(l) if l else w1_raw, ACT.Copy,
                                     scale=2.0 ** W_EXP).then_inc(w_hi, 1)

            def exponentials(c, tail):
                for jt in range(T):
                    n = c * T + jt
                    if jt % TC != DVE_SLOT:
                        if jt == TC - 1 and not tail:
                            act.wait_ge(w_split, 1)
                        act.wait_ge(rest_ready, n + 1)
                        act.nop(nofuse=True)
                        nc.scalar.activation(lr[:, jt % TC, :], sl[:, bass.ds(c * CI, CI)], ACT.Relu,
                                             bias=srs[:, 0, jt:jt + 1]).then_inc(relu_ready, 1)
                        act.wait_ge(relu_ready, c * ACT_RELUS + act_relus(jt))
                    else:
                        act.wait_ge(dve_relu_ready, c * (T - ACT_RELUS) + jt // TC + 1)
                    if jt == 0 and not tail:
                        act.wait_ge(shifted, 1)
                        nc.scalar.activation(row_eps[:, :], row_eps[:, :], ACT.Exp).then_inc(eps_ready, 1)
                    act.wait_ge(e_used, n + 1)
                    nc.scalar.activation(er[:, jt % RING, HI, :], lr[:, jt % TC, :], ACT.Exp,
                                         bias=srs[:, 1, jt:jt + 1], scale=-1.0)
                    nc.scalar.activation(lr[:, jt % TC, :], lr[:, jt % TC, :], ACT.Exp,
                                         bias=srs[:, 1, jt:jt + 1], scale=-1.0).then_inc(exp_done, 1)
                    if jt == W1_AT and not tail:
                        split_weights_hi(0)
                    if jt == W_AT and not tail:
                        for l in range(1, LAYERS):
                            split_weights_hi(l)
                    if jt == (GATE_AT if tail else GATE_0_AT):
                        squash_gates(c)
                    if jt == TANH_AT and tail:
                        squash_sum(c - 1)
                    if jt == HI_AT and tail:
                        split_hi_0(c - 1)

            def squash_gates(c):
                act.wait_ge(ab_ready, c + 1)
                act.nop(nofuse=True)
                nc.scalar.activation(gates(c), gates(c), ACT.Tanh, scale=0.5).then_inc(ab_tanh, 1)

            def squash_sum(c):
                for it in range(TC):
                    act.wait_ge(sum_ready, (c + 1) * TC + it + 1)
                    act.nop(nofuse=True)
                    nc.scalar.activation(y(c, it), y(c, it), ACT.Tanh, scale=0.5).then_inc(sum_tanh, 1)

            def split_hi_0(c):
                for it in range(TC):
                    t = c * TC + it
                    act.wait_ge(xn_ready, t + 1)
                    act.nop(nofuse=True)
                    nc.scalar.activation(xs[:, 0, HI, bass.ds(t, 1), :], x32[:, bass.ds(t, 1), :],
                                         ACT.Copy).then_inc(hi_ready, 1)

            exponentials(0, False)
            with act.Fori(1, C) as c:
                exponentials(c, True)
            squash_sum(C - 1)
            split_hi_0(C - 1)

            def evacuate(s):
                for k in range(K):
                    act.wait_ge(yt_done, K * s + k + 1)
                    nc.scalar.activation(YT[:, HI, k, :], ps[:, bass.ds((s % 2) * K + k, 1), :],
                                         ACT.Copy).then_inc(yt_hi, 1)

            def split_hi(s):
                l, c = split_step(s, LAYERS - 1)
                for it in range(TC):
                    act.wait_ge(xn_ready, T + s * TC + it + 1)
                    nc.scalar.activation(xs[:, bass.ds((l + 1) % 2, 1), HI, bass.ds(c * TC + it, 1), :],
                                         x32[:, bass.ds(c * TC + it, 1), :], ACT.Copy,
                                         scale=scale[:, bass.ds(l + 1, 1), bass.ds(c * TC + it, 1)]
                                         ).then_inc(hi_ready, 1)

            evacuate(0)
            act.wait_ge(dis_ready, 1)
            with act.Fori(1, STEPS - C + 1) as s:
                split_hi(s - 1)
                evacuate(s)
            with act.Fori(STEPS - C + 1, STEPS) as s:
                evacuate(s)

        @block.vector
        def _(dve):
            done = [0]

            class Chain:
                def __init__(self, turn=0, per=0):
                    self.base, self.per, self.k, self.turn = done[0], per, 0, turn

                def __call__(self, ins):
                    self.k += 1
                    ins.then_inc(dve_done, 1)

                def wait(self, back=0):
                    dve.wait_ge(dve_done, self.turn * self.per + (self.base + self.k - back))

                def end(self, turns=1):
                    assert turns == 1 or self.k == self.per, self.k
                    done[0] = self.base + self.k * turns

            dve.sem_inc(blocks_copied[0], 1)
            dve.sem_inc(xT_split, 1)
            dve.sem_inc(hg_split, 2)
            dve.sem_inc(sum_ready, TC)
            dve.sem_inc(rest_ready, TC)
            dve.sem_inc(sl_done, 1)
            dve.wait_ge(sa_weights, 16 * 2)
            for k in range(K):
                for side in range(2):
                    nc.vector.tensor_tensor_reduce(
                        products[:, 2 * k + side, :], wH[:, k, 0:D], a_bc[:, (1 - side) * D:(2 - side) * D], 1.0, 0.0,
                        ALU.mult, ALU.add, wH[:, k, D + side:D + side + 1]).then_inc(folded, 1)

            def take_cols(t, i):
                h = h_bank(i)
                dve.wait_ge(hg_copied, t + 1)
                nc.vector.tensor_scalar(sl_col[:, i % TC:i % TC + 1], ps[:, h, D + 1:D + 2], 2.0 ** -W_EXP, None,
                                        ALU.mult)
                nc.vector.tensor_scalar(row_eps[:, bass.ds(t, 1)], ps[:, h, D + 1:D + 2], 2.0 ** -W_EXP, None,
                                        ALU.mult)
                nc.vector.tensor_scalar(srs[:, 0, bass.ds(t, 1)], ps[:, h, D:D + 1], (1.0 - SLOPE) * 2.0 ** -W_EXP,
                                        None, ALU.mult)
                nc.vector.tensor_scalar(srs[:, 1, bass.ds(t, 1)], ps[:, h, D:D + 1], -SLOPE * 2.0 ** -W_EXP, None,
                                        ALU.mult).then_inc(cols_copied, 1)

            def take_lo(t, i):
                h, g = h_bank(i), g_bank(i)
                for out, bank, width, minus, op in (
                        (hs[:, LO, bass.ds(t, 1), 0:D], h, (0, D), hs[:, HI, bass.ds(t, 1), 0:D], ALU.subtract),
                        (vab[:, bass.ds(t, 1), :], g, (V, V + 2), bab[:, :], ALU.add),
                        (gs[:, LO, bass.ds(t, 1), 0:U + 2], g, (0, U + 2), gs[:, HI, bass.ds(t, 1), 0:U + 2],
                         ALU.subtract)):
                    ins = nc.vector.scalar_tensor_tensor(out=out, in0=ps[:, bank, width[0]:width[1]],
                                                         scalar=2.0 ** -W_EXP, in1=minus, op0=ALU.mult, op1=op)
                ins.then_inc(hg_split, 1)

            def take_x_lo(t, i):
                dve.wait_ge(xT_hi, t + 1)
                nc.vector.tensor_tensor(xT[:, i % 2, LO, :, :], ps[:, X_BANK, 0:D].rearrange("p (k n) -> p k n", k=K),
                                        xT[:, i % 2, HI, :, :], ALU.subtract).then_inc(xT_split, 1)

            def take_blocks(c, it, part=0):
                dve.wait_ge(adj_transposed, 2 * (c * TC + it) + part + 1)
                nc.vector.tensor_copy(adjT[:, bass.ds(c, 1), part * HALF:(part + 1) * HALF, it * P:(it + 1) * P],
                                      blocks(part)).then_inc(blocks_copied[part], 1)

            def load_chunk(c, last):
                for it in range(TC):
                    for i in (2 * it, 2 * it + 1):
                        if i + 1 < XS or not last:
                            take_x_lo(c * XS + i + 1, i + 1)
                        if i % TC == 0:
                            dve.wait_ge(sl_done, 2 * c + i // TC + 1)
                        take_cols(c * XS + i, i)
                        take_lo(c * XS + i, i)
                    take_blocks(c, it)

            for n, (w16, w) in enumerate(((wH16, wH), (wG16, wG))):
                dve.wait_ge(early_hi, n + 1)
                nc.vector.scalar_tensor_tensor(out=w16[:, LO, :, :], in0=w, scalar=2.0 ** W_EXP,
                                               in1=w16[:, HI, :, :], op0=ALU.mult, op1=ALU.subtract
                                               ).then_inc(early_split, 1)
                if n == 0:
                    take_x_lo(0, 0)
            dve.wait_ge(bab_loaded, 16 * 2)
            with dve.Fori(0, C // 2 - 1) as c:
                load_chunk(c, False)
            load_chunk(C // 2 - 1, True)
            dve.wait_ge(cols_copied, T)
            nc.vector.tensor_reduce(top[:, 0:1], srs[:, 1, :], mybir.AxisListType.X, ALU.max).then_inc(top_local, 1)

            dve.wait_ge(tables_ready, 1)
            dve.wait_ge(x_kept, T)
            dve.wait_ge(sl_copied, C + 1)

            def split_weights_lo(l):
                dve.wait_ge(w_hi, l + 1)
                nc.vector.scalar_tensor_tensor(out=wL[:, l, LO, :, :], in0=wt(l) if l else w1_raw,
                                               scalar=2.0 ** W_EXP, in1=wL[:, l, HI, :, :], op0=ALU.mult,
                                               op1=ALU.subtract).then_inc(w_split, 1)

            def relu(c, jt):
                dve.wait_ge(rest_ready, c * T + jt + 1)
                nc.vector.tensor_scalar(lr[:, jt % TC, :], sl[:, bass.ds(c * CI, CI)], srs[:, 0, jt:jt + 1], 0.0,
                                        ALU.add, ALU.max).then_inc(dve_relu_ready, 1)

            def shift_exponents():
                dve.wait_ge(top_spread, 1)
                nc.vector.tensor_reduce(top[:, 1:2], ps[:, TOP_BANK, 0:P], mybir.AxisListType.X, ALU.max
                                        ).then_inc(top_local, 1)
                dve.wait_ge(top_local, 2)
                nc.vector.tensor_scalar(srs[:, 1, :], srs[:, 1, :], top[:, 1:2], E_EXP * math.log(2.0), ALU.subtract,
                                        ALU.add)
                nc.vector.tensor_scalar(row_eps[:, :], row_eps[:, :], SLOPE, top[:, 1:2], ALU.mult, ALU.subtract
                                        ).then_inc(shifted, 1)

            def rest(c, jt):
                dve.wait_ge(exp_done, c * T + jt + 1)
                nc.vector.tensor_tensor(er[:, jt % RING, LO, :], lr[:, jt % TC, :], er[:, jt % RING, HI, :],
                                        ALU.subtract).then_inc(rest_ready, 1)

            def mask(c, jt):
                dve.wait_ge(rest_ready, c * T + jt + TC + 1)
                nc.vector.tensor_tensor(er[:, jt % RING, :, :], er[:, jt % RING, :, :],
                                        adjT[:, bass.ds(c, 1), jt, :].broadcast_to([P, 2, CI]),
                                        ALU.mult).then_inc(e_ready, 1)

            def take_aggregate(c, behind):
                if behind:
                    dve.wait_ge(xn_ready, (c - 1) * TC)
                dve.wait_ge(xb_done, c + 1)
                nc.vector.tensor_tensor(gates(c), ps[:, 0:TC, U:U + 2], vab[:, bass.ds(c * TC, TC), :],
                                        ALU.add).then_inc(ab_ready, 1)
                nc.vector.tensor_copy(bscale[:, 1, bass.ds(c * TC, TC)], ps[:, 0:TC, ONE])
                nc.vector.tensor_scalar(scale[:, 2, bass.ds(c * TC, TC)], ps[:, 0:TC, ONE], DEG_EPS, None,
                                        ALU.add)
                for it in range(TC):
                    nc.vector.tensor_tensor(y(c, it), ps[:, it:it + 1, 0:D], bias[:, 0:1, :],
                                            ALU.add).then_inc(xb_read, 1)

            def gate(c):
                dve.wait_ge(ab_tanh, c + 1)
                nc.vector.tensor_scalar(gates(c), gates(c), 0.5, 0.5, ALU.mult, ALU.add).then_inc(gates_ready, 1)

            def add_attention(c, chain):
                dve.wait_ge(eps_ready, 1)
                dve.wait_ge(e_used, (c + 1) * T + RING)
                chain(nc.vector.scalar_tensor_tensor(out=rd[:, :], in0=row_eps[:, bass.ds(c * TC, TC)],
                                                     scalar=DEN_EPS * 2.0 ** E_EXP, in1=ps[:, XA:XA + TC, D],
                                                     op0=ALU.mult, op1=ALU.add))
                chain.wait()
                chain(nc.vector.reciprocal(rd[:, :], rd[:, :]))
                chain.wait()
                dve.wait_ge(gates_ready, c + 1)
                chain(nc.vector.tensor_tensor(rd[:, :], rd[:, :], ab[:, bass.ds((c % 2) * TC, TC), 0], ALU.mult))
                chain.wait()
                dve.wait_ge(y_gated, (c + 1) * TC)
                for it in range(TC):
                    nc.vector.scalar_tensor_tensor(out=y(c, it), in0=ps[:, XA + it:XA + it + 1, 0:D],
                                                   scalar=rd[:, it:it + 1], in1=y(c, it),
                                                   op0=ALU.mult, op1=ALU.add).then_inc(sum_ready, 1)

            def variance_0(c, chain):
                for it in range(TC):
                    dve.wait_ge(sum_tanh, c * TC + it + 1)
                    ins = nc.vector.scalar_tensor_tensor(out=y(c, it), in0=y(c, it), scalar=0.5,
                                                         in1=x32[:, bass.ds(c * TC + it, 1), :],
                                                         op0=ALU.mult, op1=ALU.add)
                chain(ins)
                chain.wait()
                dve.nop(nofuse=True)
                for it in range(TC):
                    ins = nc.vector.bn_stats(st[:, it, :], x_in[:, bass.ds((c % 2) * TC + it, 1), :])
                chain(ins)
                chain.wait()
                dve.nop(nofuse=True)
                for it in range(TC):
                    ins = nc.vector.bn_aggr(mv[:, it, :], st[:, it, :])
                chain(ins)
                chain.wait()
                nc.vector.tensor_scalar(rs[:, :], mv[:, :, 1], LN_EPS, None, ALU.add).then_inc(var_ready, 1)

            def normalise_0(c):
                dve.wait_ge(rs_ready, c + 1)
                for it in range(TC):
                    nc.vector.tensor_scalar(x32[:, bass.ds(c * TC + it, 1), :], y(c, it), mv[:, it, 0:1],
                                            rs[:, it:it + 1], ALU.subtract, ALU.mult).then_inc(xn_ready, 1)

            def split_lo_0(c):
                for it in range(TC):
                    t = c * TC + it
                    dve.wait_ge(hi_ready, t + 1)
                    nc.vector.tensor_tensor(xs[:, 0, LO, bass.ds(t, 1), :], x32[:, bass.ds(t, 1), :],
                                            xs[:, 0, HI, bass.ds(t, 1), :], ALU.subtract).then_inc(split_ready, 1)

            def chunk_0(c, chain, tail, ahead=True):
                for jt in range(T):
                    if not tail:
                        for t in ([T // 2] if jt == 0 else []) + ([T // 2 + jt + 1] if jt < T // 2 - 1 else []):
                            for part in range(2):
                                take_blocks(t // TC, t % TC, part)
                            if t == T // 2:
                                shift_exponents()
                    if (jt + DVE_SLOT) % TC == DVE_SLOT:
                        relu(c, jt + DVE_SLOT)
                    rest(c, jt)
                    if jt > 0:
                        mask(c, jt - 1)
                    if jt == W1_AT and not tail:
                        split_weights_lo(0)
                    if jt == LOADED_AT and not tail:
                        dve.wait_ge(biases_loaded, 16 * (1 + LAYERS))
                        take_aggregate(0, False)
                    if jt == W_AT and not tail:
                        for l in range(1, LAYERS):
                            split_weights_lo(l)
                    if jt == (GATED_AT if tail else GATED_0_AT):
                        gate(c)
                    if jt == SUM_AT and tail:
                        add_attention(c - 1, chain)
                    if jt == VAR_AT and tail:
                        variance_0(c - 1, chain)
                    if jt == NORM_AT and tail:
                        normalise_0(c - 1)
                    if jt == AGG_AT and ahead:
                        take_aggregate(c + 1, tail)
                mask(c, T - 1)

            chain = Chain()
            chunk_0(0, chain, False)
            chain.end()
            with dve.Fori(1, C - 1) as c:
                chain = Chain(c - 1, 6)
                chunk_0(c, chain, True)
            chain.end(C - 2)
            chain = Chain()
            chunk_0(C - 1, chain, True, False)
            dve.wait_ge(dis_ready, 1)
            chain(nc.vector.tensor_scalar(zscale[:, 2, :], scale[:, 2, :], 2.0 ** -W_EXP, None, ALU.mult))
            add_attention(C - 1, chain)
            variance_0(C - 1, chain)
            normalise_0(C - 1)
            split_lo_0(C - 1)
            chain.end()
            def split_yt(s):
                for k in range(K):
                    dve.wait_ge(yt_hi, K * s + k + 1)
                    nc.vector.tensor_tensor(YT[:, LO, k, :], ps[:, bass.ds((s % 2) * K + k, 1), :],
                                            YT[:, HI, k, :], ALU.subtract).then_inc(yt_split, 1)

            def norm(s, chain, last):
                l, c = split_step(s, LAYERS if last else LAYERS - 1)
                pairs = [(0, 1), (2, 3)]
                dve.wait_ge(xn_ready, T + s * TC)
                for n, pair in enumerate(pairs):
                    for it in pair:
                        dve.wait_ge(z_done, s * TC + it + 1)
                        dve.wait_ge(bias_added, s * TC + it + 2)
                        chain(nc.vector.scalar_tensor_tensor(
                            out=v[:, it, :], in0=ps[:, Z_BANK + it, 0:D],
                            scalar=zscale[:, bass.ds(l, 1), bass.ds(c * TC + it, 1)],
                            in1=x32[:, bass.ds(c * TC + it, 1), :], op0=ALU.mult, op1=ALU.add))
                    for it in pair:
                        chain.wait(1 - it % 2)
                        ins = nc.vector.bn_stats(st[:, it, :], v[:, it, :])
                    chain(ins)
                    chain.wait()
                    dve.nop(nofuse=True)
                    for it in pair:
                        ins = nc.vector.bn_aggr(mv[:, it, :], st[:, it, :])
                    chain(ins)
                    chain.wait()
                    nc.vector.tensor_scalar(rs[:, 2 * n:2 * n + 2], mv[:, 2 * n:2 * n + 2, 1], LN_EPS, None,
                                            ALU.add).then_inc(var_ready, 1)
                for n, pair in enumerate(pairs):
                    dve.wait_ge(rs_ready, C + 2 * s + n + 1)
                    for it in pair:
                        nc.vector.tensor_scalar(x32[:, bass.ds(c * TC + it, 1), :], v[:, it, :], mv[:, it, 0:1],
                                                rs[:, it:it + 1], ALU.subtract, ALU.mult).then_inc(xn_ready, 1)
                for it in range(0 if last else TC):
                    t = c * TC + it
                    dve.wait_ge(hi_ready, T + s * TC + it + 1)
                    nc.vector.scalar_tensor_tensor(
                        out=xs[:, bass.ds((l + 1) % 2, 1), LO, bass.ds(t, 1), :],
                        in0=x32[:, bass.ds(t, 1), :], scalar=scale[:, bass.ds(l + 1, 1), bass.ds(t, 1)],
                        in1=xs[:, bass.ds((l + 1) % 2, 1), HI, bass.ds(t, 1), :],
                        op0=ALU.mult, op1=ALU.subtract).then_inc(split_ready, 1)

            with dve.Fori(0, STEPS - C) as s:
                chain = Chain(s, 8)
                split_yt(s)
                norm(s, chain, False)
            chain.end(STEPS - C)
            with dve.Fori(STEPS - C, STEPS) as s:
                chain = Chain(s - (STEPS - C), 8)
                split_yt(s)
                norm(s, chain, True)
            chain.end(C)

        @block.tensor
        def _(pe):
            pe.sem_inc(e_used, RING)
            pe.wait_ge(ident_ready, 3)

            def transpose_x(t, i):
                pe.wait_ge(xT_split, t + 1)
                for k in range(K):
                    ins = pe.transpose(ps[:, X_BANK, k * P:(k + 1) * P], x_in[:, i, k * P:(k + 1) * P],
                                       ident[:, :])
                ins.then_inc(x_transposed, 1)

            def h_and_G(t, i):
                pe.wait_ge(xT_split, t + 2)
                pe.wait_ge(hg_split, t + 1)
                for m, (bank, w, width) in enumerate(((h_bank(i), wH16, HW), (g_bank(i), wG16, GW))):
                    if i == 0:
                        pe.wait_ge(early_split, m + 1)
                    for k in range(K):
                        for n, (x_part, w_part) in enumerate(PARTS):
                            ins = pe.matmul(ps[:, bank, 0:width], xT[:, i % 2, x_part, k, :], w[:, w_part, k, :],
                                            start=(k == 0 and n == 0), stop=(k == K - 1 and n == len(PARTS) - 1))
                    ins.then_inc(hg_done, 1)

            def spread_s_left(q):
                pe.wait_ge(cols_copied, (q + 1) * TC)
                pe.wait_ge(sl_copied, q + 1)
                for i in range(TC):
                    ins = pe.matmul(ps[:, S_BANK, i * P:(i + 1) * P], sl_col[:, i:i + 1].broadcast_to([P, P]),
                                    ident[:, :], start=True, stop=True)
                ins.then_inc(sl_done, 1)

            def transpose_adj(c, it):
                t = c * TC + it
                pe.wait_ge(adj_loaded[it], 16 * (c + 1))
                for part in range(2):
                    pe.wait_ge(blocks_copied[part], t + 1)
                    for jt in range(part * HALF, (part + 1) * HALF):
                        ins = pe.transpose(blocks(part)[:, jt % HALF, :], adj16[:, it, jt * P:(jt + 1) * P],
                                           ident16[:, :])
                    ins.then_inc(adj_transposed, 1)

            def load_chunk(c, last):
                for it in range(TC):
                    for i in (2 * it, 2 * it + 1):
                        if i + 1 < XS or not last:
                            pe.wait_ge(x_loaded[(i + 1) % XS], 16 * (c + (i + 1) // XS + 1))
                            transpose_x(c * XS + i + 1, (i + 1) % XS)
                        h_and_G(c * XS + i, i)
                    transpose_adj(c, it)
                    if i % TC == TC - 1:
                        spread_s_left(2 * c + i // TC)

            pe.wait_ge(x_loaded[0], 16)
            transpose_x(0, 0)
            with pe.Fori(0, C // 2 - 1) as c:
                load_chunk(c, False)
            load_chunk(C // 2 - 1, True)

            def transpose_weights(l):
                for ki in range(K):
                    for ko in range(K):
                        ins = pe.transpose(wt(l)[:, ki, ko * P:(ko + 1) * P],
                                           w_raw[:, l - 1, ko, ki * P:(ki + 1) * P], ident[:, :])
                ins.then_inc(w_transposed, 1)

            def aggregate_G(c, tiles, behind=True):
                for jt in tiles:
                    for it in range(TC):
                        if jt == 0 and behind:
                            pe.wait_ge(xb_read, (c - 1) * TC + it + 1)
                        for part, width in ((HI, ONE + 1), (LO, U + 2)):
                            ins = pe.matmul(ps[:, it, 0:width], adjT[:, bass.ds(c, 1), jt, it * P:(it + 1) * P],
                                            gs[:, part, jt, 0:width], start=(jt == 0 and part == HI),
                                            stop=(jt == T - 1 and part == LO))
                return ins

            def attend(c):
                for jt in range(T):
                    pe.wait_ge(e_ready, c * T + jt + 1)
                    for it in range(TC):
                        if jt == 0:
                            pe.wait_ge(sum_ready, c * TC + it + 1)
                        for n, (e_part, h_part) in enumerate(PARTS):
                            width = D + 1 if h_part == HI else D
                            ins = pe.matmul(ps[:, XA + it, 0:width], er[:, jt % RING, e_part, it * P:(it + 1) * P],
                                            hs[:, h_part, jt, 0:width], start=(jt == 0 and n == 0),
                                            stop=(jt == T - 1 and n == len(PARTS) - 1))
                    ins.then_inc(e_used, 1)

            pe.wait_ge(hg_split, T + 2)
            pe.wait_ge(tables_ready, 1)
            for t in range(T // 2, T):
                transpose_adj(t // TC, t % TC)
                if t == T // 2:
                    pe.wait_ge(xT_split, T + 1)
                    pe.wait_ge(top_local, 1)
                    pe.matmul(ps[:, TOP_BANK, 0:P], top[:, 0:1].broadcast_to([P, P]), ident[:, :], start=True,
                              stop=True).then_inc(top_spread, 1)
                ins = aggregate_G(0, range(2 * t - T, 2 * t - T + 2), False)
            ins.then_inc(xb_done, 1)
            pe.wait_ge(square_weights, 16 * (LAYERS - 1))
            pe.wait_ge(shifted, 1)
            pe.wait_ge(sl_copied, C + 1)
            for l in range(1, LAYERS):
                transpose_weights(l)
            with pe.Fori(0, C - 1) as c:
                for part in range(2):
                    pe.wait_ge(blocks_copied[part], T + 1)
                aggregate_G(c + 1, range(T)).then_inc(xb_done, 1)
                pe.wait_ge(w_split, LAYERS)
                attend(c)
            attend(C - 1)

            def aggregate(s, k, tiles):
                l, c = split_step(s)
                for jt in tiles:
                    for part in (HI, LO):
                        ins = pe.matmul(ps[:, bass.ds((s % 2) * K + k, 1), :],
                                        xs[:, bass.ds(l % 2, 1), part, jt, k * P:(k + 1) * P],
                                        adjT[:, bass.ds(c, 1), jt, :],
                                        start=(jt == 0 and part == HI), stop=(jt == T - 1 and part == LO))
                return ins

            def project(s):
                pe.wait_ge(yt_split, K * (s + 1))
                pe.wait_ge(var_ready, C + 2 * s)
                for it in range(TC):
                    for k in range(K):
                        for n, (y_part, w_part) in enumerate(PARTS):
                            ins = pe.matmul(ps[:, Z_BANK + it, 0:D], YT[:, y_part, k, it * P:(it + 1) * P],
                                            wL[:, bass.ds(split_step(s)[0], 1), w_part, k, :],
                                            start=(k == 0 and n == 0), stop=(k == K - 1 and n == len(PARTS) - 1))
                    ins.then_inc(z_done, 1)

            START, FIRST, REST = range(TC + 2), range(T - TC), range(T - TC, T)

            def step(s, project_last):
                pe.wait_ge(split_ready, split_step(s)[0] * T + (T - TC))
                aggregate(s, 0, START)
                if project_last:
                    project(s - 1)
                aggregate(s, 0, FIRST[len(START):])
                aggregate(s, 1, FIRST)
                if not project_last:
                    for jt in REST[:-1]:
                        pe.wait_ge(split_ready, jt + 1)
                        for k in range(K):
                            aggregate(s, k, [jt])
                pe.wait_ge(split_ready, split_step(s)[0] * T + T)
                for k in range(K):
                    aggregate(s, k, REST if project_last else REST[-1:]).then_inc(yt_done, 1)

            step(0, False)
            with pe.Fori(1, STEPS) as s:
                step(s, True)
            pe.wait_ge(var_ready, C + 2 * (STEPS - 1))
            for k in range(K):
                pe.wait_ge(yt_split, K * (STEPS - 1) + k + 1)
                for it in range(TC):
                    for n, (y_part, w_part) in enumerate(PARTS):
                        ins = pe.matmul(ps[:, Z_BANK + it, 0:D], YT[:, y_part, k, it * P:(it + 1) * P],
                                        wL[:, LAYERS - 1, w_part, k, :], start=(k == 0 and n == 0),
                                        stop=(k == K - 1 and n == len(PARTS) - 1))
                    if k == K - 1:
                        ins.then_inc(z_done, 1)


_INS = ['x', 'adj', 'L0_gnn_W_sa', 'L0_gnn_a_sa', 'L0_gnn_W_gcnb', 'L0_gnn_b_gcnb', 'L0_gnn_Wa', 'L0_gnn_ba',
        'L0_gnn_Wb', 'L0_gnn_bb', 'L1_gnn_W', 'L1_gnn_b', 'L2_gnn_W', 'L2_gnn_b', 'L3_gnn_W', 'L3_gnn_b']


def kernel(**inputs):
    import numpy as _np
    import concourse.bacc as _bacc
    from concourse import mybir as _mybir
    from concourse.bass_utils import run_bass_kernel_spmd as _run

    nc = _bacc.Bacc("TRN2", target_bir_lowering=False, num_devices=1)
    arrays, args = {}, []
    for name in _INS:
        a = _np.ascontiguousarray(inputs[name])
        arrays[f"in_{name}_dram"] = a
        args.append(nc.dram_tensor(f"in_{name}_dram", a.shape, _mybir.dt.from_np(a.dtype), kind="ExternalInput").ap())
    shape = inputs['x'].shape
    args.append(nc.dram_tensor("out_0_dram", shape, _mybir.dt.float32, kind="ExternalOutput").ap())
    build(nc, *args)
    r = _run(nc, [arrays], core_ids=[0])
    return r.results[0]["out_0_dram"]
```
